# Optimizing a Trainium2 kernel written in Bass

```python
import numpy as np
import jax
import jax.numpy as jnp

def _softmax(x, axis=-1):
    return jax.nn.softmax(x, axis=axis)

def _gelu(x):
    return jax.nn.gelu(x, approximate=True)

def _silu(x):
    return jax.nn.silu(x)

def _sigmoid(x):
    return jax.nn.sigmoid(x)

def _layernorm(x, axis=-1, eps=1e-05):
    m = jnp.mean(x, axis=axis, keepdims=True)
    v = jnp.var(x, axis=axis, keepdims=True)
    return (x - m) / jnp.sqrt(v + eps)

def _scatter_add(tgt, idx, src, axis=0):
    return tgt.at[idx].add(src)

def _segment_sum(src, seg, n):
    return jax.ops.segment_sum(src, seg, n)
kernel_name = 'mk_cond_seq_d4_seqx_r4_6dd6c8'

def setup_inputs(seed: int=0):
    np.random.seed(seed)
    _w = jnp.asarray

    def _rec_inputs():
        import jax
        import jax.numpy as jnp
        _rk = jax.random.key(seed)
        x = 1.648e-05 + 1 * jax.random.normal(jax.random.fold_in(_rk, 1), (8, 256, 288), jnp.float32)
        _lenS = 256 - jax.random.randint(jax.random.fold_in(_rk, 7), (8,), 0, max(1, 256 // 4) + 1, jnp.int32)
        _lenS2 = 256 - jax.random.randint(jax.random.fold_in(_rk, 8), (8,), 0, max(1, 256 // 4) + 1, jnp.int32)
        cond_1152 = 0.00914911 + 1.00357 * jax.random.normal(jax.random.fold_in(_rk, 11), (8, 288), jnp.float32)
        return (x, cond_1152)
    x, cond_1152 = _rec_inputs()

    def _L0_cond_setup():
        import jax, jax.numpy as jnp
        import numpy as np
        NUM_HEADS = 16
        NUM_EXPERTS = 4
        TOP_K = 2
        LN_EPS = 1e-06

        def _ln(h):
            mu = jnp.mean(h, axis=-1, keepdims=True)
            var = jnp.var(h, axis=-1, keepdims=True)
            return (h - mu) * jax.lax.rsqrt(var + LN_EPS)

        def _modulate(h, shift, scale):
            return h * (1.0 + scale[:, None, :]) + shift[:, None, :]
        key = jax.random.key(seed)
        ks = jax.random.split(key, 12)
        B, N, C = (8, 256, 288)
        H = 4 * C
        E = NUM_EXPERTS
        s = 0.02
        return {'x': jax.random.normal(ks[0], (B, N, C), jnp.float32), 'c': jax.random.normal(ks[1], (B, C), jnp.float32), 'w_adaln': jax.random.normal(ks[2], (C, 6 * C), jnp.float32) * s, 'b_adaln': jnp.zeros((6 * C,), jnp.float32), 'w_qkv': jax.random.normal(ks[3], (C, 3 * C), jnp.float32) * s, 'b_qkv': jnp.zeros((3 * C,), jnp.float32), 'w_proj': jax.random.normal(ks[4], (C, C), jnp.float32) * s, 'b_proj': jnp.zeros((C,), jnp.float32), 'w_gate': jax.random.normal(ks[5], (C, E), jnp.float32) * s, 'w1': jax.random.normal(ks[6], (E, C, H), jnp.float32) * s, 'b1': jnp.zeros((E, H), jnp.float32), 'w2': jax.random.normal(ks[7], (E, H, C), jnp.float32) * s, 'b2': jnp.zeros((E, C), jnp.float32)}
    _L0_cond_all = _L0_cond_setup()
    _L0_cond_in = {k: v for k, v in _L0_cond_all.items() if k in ('w_adaln', 'b_adaln', 'w_qkv', 'b_qkv', 'w_proj', 'b_proj', 'w_gate', 'w1', 'b1', 'w2', 'b2')}
    del _L0_cond_all

    def _L1_cond_setup():
        import jax, jax.numpy as jnp
        import numpy as np
        N, T, D, H = (32, 256, 288, 16)
        DH = D // H
        MLP = int(D * 4.0)
        EPS = 1e-06

        def _layernorm(x):
            m = jnp.mean(x, axis=-1, keepdims=True)
            v = jnp.var(x, axis=-1, keepdims=True)
            return (x - m) * jax.lax.rsqrt(v + EPS)

        def _modulate(x, shift, scale):
            return x * (1.0 + scale[:, None, :]) + shift[:, None, :]

        def _attention(x, qkv_w, qkv_b, proj_w, proj_b):
            n, t, d = x.shape
            scale = DH ** (-0.5)
            qkv = x @ qkv_w + qkv_b
            qkv = qkv.reshape(n, t, 3, H, DH)
            q, k, v = (qkv[:, :, 0], qkv[:, :, 1], qkv[:, :, 2])
            attn = jnp.einsum('nthd,ntkd->nthk', q * scale, k)
            attn = jax.nn.softmax(attn, axis=-1)
            out = jnp.einsum('nthk,ntkd->nthd', attn, v)
            out = out.transpose(0, 2, 1, 3).reshape(n, t, d)
            return out @ proj_w + proj_b

        def _mlp(x, fc1_w, fc1_b, fc2_w, fc2_b):
            h = jax.nn.gelu(x @ fc1_w + fc1_b, approximate=False)
            return h @ fc2_w + fc2_b
        key = jax.random.key(seed)
        ks = jax.random.split(key, 14)
        s = 0.02
        return {'x': jax.random.normal(ks[0], (N, T, D), jnp.float32), 'c': jax.random.normal(ks[1], (N, D), jnp.float32), 'qkv_w': jax.random.normal(ks[2], (D, 3 * D), jnp.float32) * s, 'qkv_b': jax.random.normal(ks[3], (3 * D,), jnp.float32) * s, 'proj_w': jax.random.normal(ks[4], (D, D), jnp.float32) * s, 'proj_b': jax.random.normal(ks[5], (D,), jnp.float32) * s, 'fc1_w': jax.random.normal(ks[6], (D, MLP), jnp.float32) * s, 'fc1_b': jax.random.normal(ks[7], (MLP,), jnp.float32) * s, 'fc2_w': jax.random.normal(ks[8], (MLP, D), jnp.float32) * s, 'fc2_b': jax.random.normal(ks[9], (D,), jnp.float32) * s, 'ada_w': jax.random.normal(ks[10], (D, 6 * D), jnp.float32) * s, 'ada_b': jax.random.normal(ks[11], (6 * D,), jnp.float32) * s}
    _L1_cond_all = _L1_cond_setup()
    _L1_cond_in = {k: v for k, v in _L1_cond_all.items() if k in ('qkv_w', 'qkv_b', 'proj_w', 'proj_b', 'fc1_w', 'fc1_b', 'fc2_w', 'fc2_b', 'ada_w', 'ada_b')}
    del _L1_cond_all

    def _L2_cond_setup():
        import jax, jax.numpy as jnp
        import numpy as np
        B, L, C = (8, 256, 288)
        H = 16
        D = C // H
        FF = int(C * 4.0)
        EPS = 1e-06

        def _layernorm(x):
            mu = jnp.mean(x, axis=-1, keepdims=True)
            var = jnp.mean(jnp.square(x - mu), axis=-1, keepdims=True)
            return (x - mu) * jax.lax.rsqrt(var + EPS)

        def _modulate(x, shift, scale):
            return x * (1.0 + scale) + shift

        def _attention(h, W_qkv, b_qkv, W_proj, b_proj):
            b, l, c = h.shape
            qkv = h @ W_qkv + b_qkv
            qkv = qkv.reshape(b, l, 3, H, D)
            q, k, v = (qkv[:, :, 0], qkv[:, :, 1], qkv[:, :, 2])
            scale = D ** (-0.5)
            scores = jnp.einsum('blhd,bmhd->bhlm', q * scale, k)
            attn = jax.nn.softmax(scores, axis=-1)
            o = jnp.einsum('bhlm,bmhd->blhd', attn, v).reshape(b, l, c)
            return o @ W_proj + b_proj
        key = jax.random.key(seed)
        ks = jax.random.split(key, 12)
        s = 0.02
        return {'x': jax.random.normal(ks[0], (B, L, C), jnp.float32), 'c': jax.random.normal(ks[1], (B, 1, C), jnp.float32), 'W_qkv': jax.random.normal(ks[2], (C, 3 * C), jnp.float32) * s, 'b_qkv': jnp.zeros((3 * C,), jnp.float32), 'W_proj': jax.random.normal(ks[3], (C, C), jnp.float32) * s, 'b_proj': jnp.zeros((C,), jnp.float32), 'W_fc1': jax.random.normal(ks[4], (C, FF), jnp.float32) * s, 'b_fc1': jnp.zeros((FF,), jnp.float32), 'W_fc2': jax.random.normal(ks[5], (FF, C), jnp.float32) * s, 'b_fc2': jnp.zeros((C,), jnp.float32), 'W_ada': jax.random.normal(ks[6], (C, 6 * C), jnp.float32) * s, 'b_ada': jnp.zeros((6 * C,), jnp.float32)}
    _L2_cond_all = _L2_cond_setup()
    _L2_cond_in = {k: v for k, v in _L2_cond_all.items() if k in ('W_qkv', 'b_qkv', 'W_proj', 'b_proj', 'W_fc1', 'b_fc1', 'W_fc2', 'b_fc2', 'W_ada', 'b_ada')}
    del _L2_cond_all

    def _L3_cond_setup():
        import jax, jax.numpy as jnp
        import numpy as np
        from jax.scipy.linalg import expm
        N, D, COND_DIM = (288, 64, 288)
        B, T = (16, 256)

        def _rotation(cond, W, b):
            v = jax.nn.silu(cond) @ W.T + b
            iu, ju = jnp.triu_indices(D, k=1)
            A = jnp.zeros((cond.shape[0], D, D), dtype=v.dtype)
            A = A.at[:, iu, ju].set(v).at[:, ju, iu].set(-v)
            return expm(A)
        key = jax.random.key(seed)
        k1, k2, k3, k4, k5 = jax.random.split(key, 5)
        x = jax.random.normal(k1, (B, T, N), dtype=jnp.float32)
        cond = jax.random.normal(k2, (B, COND_DIM), dtype=jnp.float32)
        P = jax.random.normal(k3, (N, D), dtype=jnp.float32)
        n_skew = D * (D - 1) // 2
        bound = 1.0 / np.sqrt(COND_DIM)
        W = jax.random.uniform(k4, (n_skew, COND_DIM), minval=-bound, maxval=bound, dtype=jnp.float32)
        b = jax.random.uniform(k5, (n_skew,), minval=-bound, maxval=bound, dtype=jnp.float32)
        return {'x': x, 'cond': cond, 'P': P, 'W': W, 'b': b}
    _L3_cond_all = _L3_cond_setup()
    _L3_cond_in = {k: v for k, v in _L3_cond_all.items() if k in ('P', 'W', 'b')}
    del _L3_cond_all
    return {'x': x, 'cond_1152': cond_1152, 'L0_cond_w_adaln': _L0_cond_in['w_adaln'], 'L0_cond_b_adaln': _L0_cond_in['b_adaln'], 'L0_cond_w_qkv': _L0_cond_in['w_qkv'], 'L0_cond_b_qkv': _L0_cond_in['b_qkv'], 'L0_cond_w_proj': _L0_cond_in['w_proj'], 'L0_cond_b_proj': _L0_cond_in['b_proj'], 'L0_cond_w_gate': _L0_cond_in['w_gate'], 'L0_cond_w1': _L0_cond_in['w1'], 'L0_cond_b1': _L0_cond_in['b1'], 'L0_cond_w2': _L0_cond_in['w2'], 'L0_cond_b2': _L0_cond_in['b2'], 'L1_cond_qkv_w': _L1_cond_in['qkv_w'], 'L1_cond_qkv_b': _L1_cond_in['qkv_b'], 'L1_cond_proj_w': _L1_cond_in['proj_w'], 'L1_cond_proj_b': _L1_cond_in['proj_b'], 'L1_cond_fc1_w': _L1_cond_in['fc1_w'], 'L1_cond_fc1_b': _L1_cond_in['fc1_b'], 'L1_cond_fc2_w': _L1_cond_in['fc2_w'], 'L1_cond_fc2_b': _L1_cond_in['fc2_b'], 'L1_cond_ada_w': _L1_cond_in['ada_w'], 'L1_cond_ada_b': _L1_cond_in['ada_b'], 'L2_cond_W_qkv': _L2_cond_in['W_qkv'], 'L2_cond_b_qkv': _L2_cond_in['b_qkv'], 'L2_cond_W_proj': _L2_cond_in['W_proj'], 'L2_cond_b_proj': _L2_cond_in['b_proj'], 'L2_cond_W_fc1': _L2_cond_in['W_fc1'], 'L2_cond_b_fc1': _L2_cond_in['b_fc1'], 'L2_cond_W_fc2': _L2_cond_in['W_fc2'], 'L2_cond_b_fc2': _L2_cond_in['b_fc2'], 'L2_cond_W_ada': _L2_cond_in['W_ada'], 'L2_cond_b_ada': _L2_cond_in['b_ada'], 'L3_cond_P': _L3_cond_in['P'], 'L3_cond_W': _L3_cond_in['W'], 'L3_cond_b': _L3_cond_in['b']}

def reference(x, cond_1152, L0_cond_w_adaln, L0_cond_b_adaln, L0_cond_w_qkv, L0_cond_b_qkv, L0_cond_w_proj, L0_cond_b_proj, L0_cond_w_gate, L0_cond_w1, L0_cond_b1, L0_cond_w2, L0_cond_b2, L1_cond_qkv_w, L1_cond_qkv_b, L1_cond_proj_w, L1_cond_proj_b, L1_cond_fc1_w, L1_cond_fc1_b, L1_cond_fc2_w, L1_cond_fc2_b, L1_cond_ada_w, L1_cond_ada_b, L2_cond_W_qkv, L2_cond_b_qkv, L2_cond_W_proj, L2_cond_b_proj, L2_cond_W_fc1, L2_cond_b_fc1, L2_cond_W_fc2, L2_cond_b_fc2, L2_cond_W_ada, L2_cond_b_ada, L3_cond_P, L3_cond_W, L3_cond_b):
    import jax
    import jax.numpy as jnp

    def _L0_cond_ref(x, c, w_adaln, b_adaln, w_qkv, b_qkv, w_proj, b_proj, w_gate, w1, b1, w2, b2):
        import jax, jax.numpy as jnp
        import numpy as np
        NUM_HEADS = 16
        NUM_EXPERTS = 4
        TOP_K = 2
        LN_EPS = 1e-06

        def _ln(h):
            mu = jnp.mean(h, axis=-1, keepdims=True)
            var = jnp.var(h, axis=-1, keepdims=True)
            return (h - mu) * jax.lax.rsqrt(var + LN_EPS)

        def _modulate(h, shift, scale):
            return h * (1.0 + scale[:, None, :]) + shift[:, None, :]
        B, N, C = x.shape
        nh = NUM_HEADS
        hd = C // nh
        mod = jax.nn.silu(c) @ w_adaln + b_adaln
        sh_msa, sc_msa, g_msa, sh_mlp, sc_mlp, g_mlp = jnp.split(mod, 6, axis=-1)
        h = _modulate(_ln(x), sh_msa, sc_msa)
        qkv = (h @ w_qkv + b_qkv).reshape(B, N, 3, nh, hd).transpose(2, 0, 3, 1, 4)
        q, k, v = (qkv[0], qkv[1], qkv[2])
        attn = jax.nn.softmax(jnp.einsum('bhqd,bhkd->bhqk', q, k) * hd ** (-0.5), axis=-1)
        o = jnp.einsum('bhqk,bhkd->bhqd', attn, v).transpose(0, 2, 1, 3).reshape(B, N, C)
        o = o @ w_proj + b_proj
        x = x + g_msa[:, None, :] * o
        xn = _modulate(_ln(x), sh_mlp, sc_mlp)
        xf = xn.reshape(-1, C)
        gate_logits = xf @ w_gate
        topk_logits, topk_idx = jax.lax.top_k(gate_logits, TOP_K)
        gates = jax.nn.softmax(topk_logits, axis=-1)
        cw = jnp.sum(jax.nn.one_hot(topk_idx, NUM_EXPERTS, dtype=xf.dtype) * gates[..., None], axis=1)
        hmid = jax.nn.gelu(jnp.einsum('tc,ech->eth', xf, w1) + b1[:, None, :], approximate=True)
        eo = jnp.einsum('eth,ehc->etc', hmid, w2) + b2[:, None, :]
        moe = jnp.einsum('te,etc->tc', cw, eo).reshape(B, N, C)
        return x + g_mlp[:, None, :] * moe

    def _L1_cond_ref(x, c, qkv_w, qkv_b, proj_w, proj_b, fc1_w, fc1_b, fc2_w, fc2_b, ada_w, ada_b):
        import jax, jax.numpy as jnp
        import numpy as np
        N, T, D, H = (32, 256, 288, 16)
        DH = D // H
        MLP = int(D * 4.0)
        EPS = 1e-06

        def _layernorm(x):
            m = jnp.mean(x, axis=-1, keepdims=True)
            v = jnp.var(x, axis=-1, keepdims=True)
            return (x - m) * jax.lax.rsqrt(v + EPS)

        def _modulate(x, shift, scale):
            return x * (1.0 + scale[:, None, :]) + shift[:, None, :]

        def _attention(x, qkv_w, qkv_b, proj_w, proj_b):
            n, t, d = x.shape
            scale = DH ** (-0.5)
            qkv = x @ qkv_w + qkv_b
            qkv = qkv.reshape(n, t, 3, H, DH)
            q, k, v = (qkv[:, :, 0], qkv[:, :, 1], qkv[:, :, 2])
            attn = jnp.einsum('nthd,ntkd->nthk', q * scale, k)
            attn = jax.nn.softmax(attn, axis=-1)
            out = jnp.einsum('nthk,ntkd->nthd', attn, v)
            out = out.transpose(0, 2, 1, 3).reshape(n, t, d)
            return out @ proj_w + proj_b

        def _mlp(x, fc1_w, fc1_b, fc2_w, fc2_b):
            h = jax.nn.gelu(x @ fc1_w + fc1_b, approximate=False)
            return h @ fc2_w + fc2_b
        ada = jax.nn.silu(c) @ ada_w + ada_b
        shift_msa, scale_msa, gate_msa, shift_mlp, scale_mlp, gate_mlp = jnp.split(ada, 6, axis=1)
        x = x + gate_msa[:, None, :] * _attention(_modulate(_layernorm(x), shift_msa, scale_msa), qkv_w, qkv_b, proj_w, proj_b)
        x = x + gate_mlp[:, None, :] * _mlp(_modulate(_layernorm(x), shift_mlp, scale_mlp), fc1_w, fc1_b, fc2_w, fc2_b)
        return x

    def _L2_cond_ref(x, c, W_qkv, b_qkv, W_proj, b_proj, W_fc1, b_fc1, W_fc2, b_fc2, W_ada, b_ada):
        import jax, jax.numpy as jnp
        import numpy as np
        B, L, C = (8, 256, 288)
        H = 16
        D = C // H
        FF = int(C * 4.0)
        EPS = 1e-06

        def _layernorm(x):
            mu = jnp.mean(x, axis=-1, keepdims=True)
            var = jnp.mean(jnp.square(x - mu), axis=-1, keepdims=True)
            return (x - mu) * jax.lax.rsqrt(var + EPS)

        def _modulate(x, shift, scale):
            return x * (1.0 + scale) + shift

        def _attention(h, W_qkv, b_qkv, W_proj, b_proj):
            b, l, c = h.shape
            qkv = h @ W_qkv + b_qkv
            qkv = qkv.reshape(b, l, 3, H, D)
            q, k, v = (qkv[:, :, 0], qkv[:, :, 1], qkv[:, :, 2])
            scale = D ** (-0.5)
            scores = jnp.einsum('blhd,bmhd->bhlm', q * scale, k)
            attn = jax.nn.softmax(scores, axis=-1)
            o = jnp.einsum('bhlm,bmhd->blhd', attn, v).reshape(b, l, c)
            return o @ W_proj + b_proj
        ada = jax.nn.silu(c) @ W_ada + b_ada
        shift_msa, scale_msa, gate_msa, shift_mlp, scale_mlp, gate_mlp = jnp.split(ada, 6, axis=-1)
        h = _modulate(_layernorm(x), shift_msa, scale_msa)
        x = x + gate_msa * _attention(h, W_qkv, b_qkv, W_proj, b_proj)
        h = _modulate(_layernorm(x), shift_mlp, scale_mlp)
        mlp = jax.nn.gelu(h @ W_fc1 + b_fc1, approximate=True) @ W_fc2 + b_fc2
        x = x + gate_mlp * mlp
        return x

    def _L3_cond_ref(x, cond, P, W, b):
        import jax, jax.numpy as jnp
        import numpy as np
        from jax.scipy.linalg import expm
        N, D, COND_DIM = (288, 64, 288)
        B, T = (16, 256)

        def _rotation(cond, W, b):
            v = jax.nn.silu(cond) @ W.T + b
            iu, ju = jnp.triu_indices(D, k=1)
            A = jnp.zeros((cond.shape[0], D, D), dtype=v.dtype)
            A = A.at[:, iu, ju].set(v).at[:, ju, iu].set(-v)
            return expm(A)
        U, _ = jnp.linalg.qr(P)
        R = _rotation(cond, W, b)
        z = jnp.einsum('btn,nd->btd', x, U)
        z_rot = jnp.einsum('btd,bde->bte', z, R)
        x_rot = x + jnp.einsum('btd,nd->btn', z_rot - z, U)
        return x_rot
    x = _L0_cond_ref(x, cond_1152, L0_cond_w_adaln, L0_cond_b_adaln, L0_cond_w_qkv, L0_cond_b_qkv, L0_cond_w_proj, L0_cond_b_proj, L0_cond_w_gate, L0_cond_w1, L0_cond_b1, L0_cond_w2, L0_cond_b2)
    x = _L1_cond_ref(x, cond_1152, L1_cond_qkv_w, L1_cond_qkv_b, L1_cond_proj_w, L1_cond_proj_b, L1_cond_fc1_w, L1_cond_fc1_b, L1_cond_fc2_w, L1_cond_fc2_b, L1_cond_ada_w, L1_cond_ada_b)
    x = _L2_cond_ref(x, cond_1152[:, None, :], L2_cond_W_qkv, L2_cond_b_qkv, L2_cond_W_proj, L2_cond_b_proj, L2_cond_W_fc1, L2_cond_b_fc1, L2_cond_W_fc2, L2_cond_b_fc2, L2_cond_W_ada, L2_cond_b_ada)
    x = _L3_cond_ref(x, cond_1152, L3_cond_P, L3_cond_W, L3_cond_b)
    return x

_drawn_inputs = setup_inputs


def setup_inputs(seed=0):
    import zlib

    import numpy as np

    out = dict(_drawn_inputs(seed))
    spreads = {'L0_cond_b_adaln': (0.0, 0.43),
     'L0_cond_b_qkv': (0.0, 0.8),
     'L0_cond_b_proj': (0.0, 0.355),
     'L0_cond_b1': (0.0, 0.8),
     'L0_cond_b2': (0.0, 0.512),
     'L2_cond_b_qkv': (0.0, 0.8),
     'L2_cond_b_proj': (0.0, 0.332),
     'L2_cond_b_fc1': (0.0, 0.8),
     'L2_cond_b_fc2': (0.0, 0.357),
     'L2_cond_b_ada': (0.0, 0.377)}
    factors = {'L0_cond_w_qkv': 8.0,
     'L0_cond_w_proj': 5.574,
     'L0_cond_w_gate': 2.876,
     'L0_cond_w1': 2.707,
     'L1_cond_qkv_w': 8.0,
     'L1_cond_qkv_b': 8.0,
     'L1_cond_proj_w': 8.0,
     'L1_cond_proj_b': 25.796,
     'L1_cond_fc1_b': 64.0,
     'L1_cond_fc2_b': 24.053,
     'L1_cond_ada_b': 8.0,
     'L2_cond_W_qkv': 8.0,
     'L2_cond_W_proj': 5.458,
     'L1_cond_fc1_w': 3.222,
     'L1_cond_fc2_w': 2.961,
     'L2_cond_W_fc1': 3.063}
    for name, (base, spread) in spreads.items():
        noise = np.random.default_rng([zlib.crc32(name.encode()), seed]).standard_normal(out[name].shape)
        drawn = base * np.exp(spread * noise) if base else spread * noise
        out[name] = jnp.asarray(drawn.astype(out[name].dtype))
    for name, factor in factors.items():
        out[name] = (out[name] * factor).astype(out[name].dtype)
    return out
```

```python
from contextlib import ExitStack

import numpy as np
import concourse.bass as bass
from concourse import mybir

F32 = mybir.dt.float32
F16 = mybir.dt.float16
ALU = mybir.AluOpType
ACT = mybir.ActivationFunctionType
AX = mybir.AxisListType

B, T, C, NH, HD, HID, NE = 8, 256, 288, 16, 18, 1152, 4
NT = B * T // 128
WS = 64.0
QS = float(HD) ** -0.5
EPS = 1e-6
D = 64
NSQ = 12
PRODUCTS = [(0, 0), (1, 1), (2, 2), (3, 0), (4, 1), (0, 3), (1, 4)]


class Engine:

    def __init__(self, name, sem):
        self.name, self.sem, self.count, self.seen, self.queue = name, sem, 0, {}, []


def flat(deps):
    for d in deps:
        if d is None:
            continue
        if isinstance(d, list) or not (len(d) == 2 and isinstance(d[1], int)):
            yield from flat(d)
        else:
            yield d


class Ring:

    def __init__(self, items):
        self.items, self.free, self.at = items, [[] for _ in items], 0

    def take(self):
        i = self.at
        self.at = (i + 1) % len(self.items)
        return i, self.items[i], self.free[i]


def steps(main, *sides):
    due = [0.0] * len(sides)
    for _ in main:
        for n, (g, pace) in enumerate(sides):
            due[n] += pace
            while due[n] >= 1:
                due[n] -= 1
                if next(g, "end") == "end":
                    due[n] = -1e9
        yield


def chain(*parts):
    for p in parts:
        yield from p


def run(g):
    for _ in g:
        pass


def program(nc, I, out, scr_ada, scr_v, scr_o, stop=None):
    ctx = ExitStack()
    with ctx:
        def sb(name, shape, dt=F32):
            return ctx.enter_context(nc.sbuf_tensor(name, shape, dt))

        def sem(name):
            return ctx.enter_context(nc.semaphore(name))

        eng = {n: Engine(n, sem(f"s_{n}")) for n in ("tensor", "vector", "scalar", "gpsimd", "sync")}
        pe, dve, act, pool, sp = (eng[n] for n in ("tensor", "vector", "scalar", "gpsimd", "sync"))

        def put(e, fn, deps, inc):
            waits = []
            for s, v in flat(deps):
                if e.seen.get(id(s), 0) < v:
                    e.seen[id(s)] = v
                    waits.append((s, v))
            best = {}
            for s, v in waits:
                best[id(s)] = (s, v)
            e.queue.append((list(best.values()), fn, inc))

        def op(e, fn, *deps):
            e.count += 1
            put(e, fn, deps, (e.sem, 1))
            return (e.sem, e.count)

        def quiet(e, fn, *deps):
            put(e, fn, deps, None)

        class Dma:

            def __init__(self, name):
                self.sem, self.count = sem(name), 0

            def go(self, e, dst, src, *deps, **how):
                self.count += 16
                put(e, lambda q, dst=dst, src=src: q.dma_start(dst, src, **how), deps, (self.sem, 16))
                return (self.sem, self.count)

        def mms(items, *deps):
            n = len(items)
            for k, (o, l, r) in enumerate(items):
                fn = lambda q, o=o, l=l, r=r, a=(k == 0), z=(k == n - 1): q.matmul(o, l, r, start=a, stop=z)
                if k == n - 1:
                    return op(pe, fn, deps if k == 0 else [])
                quiet(pe, fn, deps if k == 0 else [])

        def last():
            return [(e.sem, e.count) for e in (pe, dve, act, pool) if e.count]

        X = sb("X", [128, NT, C])
        XT = sb("XT", [128, 5, NT * 128], F16)
        W1 = [sb(f"W1_{i}", [128, 5, HID], F16) for i in range(2)]
        W2 = sb("W2", [128, 9, 2, C], F16)
        WQ = sb("WQ", [128, 5, 3 * C], F16)
        WP = sb("WP", [128, 5, C], F16)
        WG = sb("WG", [128, 5, NE], F16)
        STG = [sb(f"STG{i}", [128, 1152]) for i in range(2)]
        ADB = sb("ADB", [128, 10 * C])
        AD1 = [ADB[:, 2 * i * C:(2 * i + 2) * C] for i in range(2)]
        AD2 = [ADB[:, (4 + 3 * i) * C:(7 + 3 * i) * C] for i in range(2)]
        H = sb("H", [128, 2, 9 * 2 * 512], F16)
        QT = [sb(f"QT{i}", [128, 8, 256], F16) for i in range(2)]
        KZ = [sb(f"KZ{i}", [128, 8, 2, 256], F16) for i in range(2)]
        VB = [sb(f"VB{i}", [128, 2, NH, 37], F16) for i in range(2)]
        QB = sb("QB", [128, NH, 64], F16)
        KB = sb("KB", [128, NH, 64], F16)
        G32 = [sb(f"G32_{i}", [128, 512]) for i in range(2)]
        TM = [sb(f"TM{i}", [128, C]) for i in range(2)]
        GB = sb("GB", [128, C])
        BQ = sb("BQ", [128, 3 * C])
        BP = sb("BP", [128, C])
        B2 = sb("B2", [128, NE, C])
        B1 = sb("B1", [128, NE, 9])
        CT = sb("CT", [96, 3, B])
        CS = sb("CS", [96, 3, B])
        OSM = sb("OSM", [96, 2 * C])
        OS = [OSM[0:B, i * C:(i + 1) * C] for i in range(2)]
        IDF = sb("IDF", [128, 128])
        IDH = sb("IDH", [128, 128], F16)
        ID2 = sb("ID2", [128, D])
        STS = [sb(f"ST{w}", [128, 2, 6]) for w in range(2)]
        MVS = [sb(f"MV{w}", [128, 2, 2]) for w in range(2)]
        RSS = [sb(f"RS{w}", [128, 2, 2]) for w in range(2)]
        PH = sb("PH", [128, 2])
        NM = sb("NM", [128, 2, 2, 8], F16)
        MT = sb("MT", [16, 256], F16)
        DN = sb("DN", [128, 4, 8])
        LG = sb("LG", [128, NT, NE])
        CW = sb("CW", [128, NT, NE])
        CWS = sb("CWS", [128, NT, NE])
        LT = sb("LT", [128, 16, 16])
        LM = sb("LM", [128, 16, 16])
        TRI = sb("TRI", [128, 16])
        L1 = sb("L1", [128, 16])
        EX = sb("EX", [128, 4, 2, D])
        EY = sb("EY", [128, 4, 2, D])
        EW = sb("EW", [128, 4, 3, D])
        AT = sb("AT", [D, C])
        TI = sb("TI", [D, D])
        NMK = sb("NMK", [D, D])
        HS = sb("HS", [D, 8])
        N2 = sb("N2", [D, 2])
        UT = sb("UT", [128, C])
        WU = sb("WU", [128, 5, D], F16)

        arena = H[:, :, :].rearrange("p a b -> p (a b)")
        used = [0]

        def over(shape, dt=F32):
            n = int(np.prod(shape)) * (2 if dt == F32 else 1)
            a = arena[:, used[0]:used[0] + n]
            used[0] += n
            if dt == F32:
                a = a.bitcast(F32)
            if len(shape) == 2:
                a = a.rearrange("p (a b) -> p a b", b=shape[1])
            elif len(shape) == 3:
                a = a.rearrange("p (a b c) -> p a b c", b=shape[1], c=shape[2])
            elif len(shape) == 4:
                a = a.rearrange("p (a b c d) -> p a b c d", b=shape[1], c=shape[2], d=shape[3])
            return a

        E32 = [over([1024]) for _ in range(2)]
        PHI = [over([2, 2, 256], F16) for _ in range(2)]
        PLO = [over([2, 2, 256], F16) for _ in range(2)]
        Y = [over([3 * C]) for _ in range(2)]
        XB = [over([2, 640], F16) for _ in range(2)]
        YL = [over([2, C]) for _ in range(2)]
        YO = over([2, C])
        ON = sb("ON", [128, 4, 2, 4 * HD])
        assert used[0] <= 2 * 9 * 2 * 512, used[0]
        small = arena[:, 0:8192].bitcast(F32)
        rHB = Ring([small[:, i * 1152:(i + 1) * 1152] for i in range(3)])
        SC = small[:, 3456:3712].rearrange("p (h k) -> p h k", k=NH)
        SM = small[:, 3712:3744]
        MB = arena[:, 0:2 * B * C].bitcast(F32).rearrange("p (b c) -> p b c", c=C)
        Hh = [H[:, i, :].rearrange("p (m s t) -> p m s t", m=9, s=2) for i in range(2)]

        PA = [ctx.enter_context(nc.psum_tensor(f"PA{i}", [128, 1024], F32)) for i in range(2)]
        PB = [ctx.enter_context(nc.psum_tensor(f"PB{i}", [128, 512], F32)) for i in range(2)]
        PC = [ctx.enter_context(nc.psum_tensor(f"PC{i}", [128, 512], F32)) for i in range(2)]
        rA, rC = Ring([p[:, :] for p in PA]), Ring([PC[0][:, :], PC[1][:, :], PB[0][:, :]])
        rO, rS = Ring([PB[1][:, :]]), Ring([PC[1][:, :]])
        rA4 = Ring([PA[0][:, 0:512], PA[0][:, 512:1024], PA[1][:, 0:512], PA[1][:, 512:1024]])
        rF = Ring([PB[0][:, :], PC[0][:, :], PB[1][:, :]])
        rXB, rY, rYL = [Ring([x]) for x in XB], Ring(Y), [Ring([y]) for y in YL]
        rE, rTM, rG, rOS = Ring([0, 1]), Ring([t[:, :] for t in TM]), Ring([g[:, :] for g in G32]), Ring(OS)
        rSTG = Ring([0, 1])
        d_stg = [Dma(f"d_stg{i}") for i in range(2)]
        d_os = [Dma(f"d_os{i}") for i in range(2)]
        d_ad = [Dma(f"d_ad{i}") for i in range(2)]
        d_ae = [Dma(f"d_ae{i}") for i in range(2)]
        d_mt = [Dma(f"d_mt{i}") for i in range(2)]
        d_ho = [Dma(f"d_ho{i}") for i in range(2)]
        d_yo = Dma("d_yo")
        d_out = [Dma(f"d_out{i}") for i in range(2)]
        d_in, d_bias, d_v, d_p, d_g2, d_c = Dma("d_in"), Dma("d_bias"), Dma("d_v"), Dma("d_p"), Dma("d_g2"), Dma("d_c")

        XW = [[] for _ in range(NT)]
        XR = [[] for _ in range(NT)]
        TW = [[] for _ in range(NT)]
        TR = [[] for _ in range(NT)]

        k = [op(pool, lambda q: q.memset(IDF[:, :], 0.0)), op(pool, lambda q: q.memset(NMK[:, :], 0.0)),
             op(pool, lambda q: q.memset(TRI[:, :], 0.0)), op(pool, lambda q: q.memset(ID2[:, :], 0.0)),
             op(pool, lambda q: q.memset(PH[:, :], -0.5))]
        t_idf = op(pool, lambda q: q.affine_select(out=IDF[:, :], in_=IDF[:, :], compare_op=ALU.not_equal, fill=1.0,
                                                   base=0, pattern=[[-1, 128]], channel_multiplier=1), k)
        t_nmk = op(pool, lambda q: q.affine_select(out=NMK[:, :], in_=NMK[:, :], compare_op=ALU.is_ge, fill=-1.0,
                                                   base=0, pattern=[[1, D]], channel_multiplier=-1), k)
        t_tri = op(pool, lambda q: q.affine_select(
            out=TRI[:, :].rearrange("p (e j) -> p e j", e=4), in_=TRI[:, :].rearrange("p (e j) -> p e j", e=4),
            compare_op=ALU.is_ge, fill=1.0, base=0, pattern=[[-1, 4], [1, 4]], channel_multiplier=0), k)
        t_id2 = op(pool, lambda q: q.affine_select(out=ID2[:, :], in_=ID2[:, :], compare_op=ALU.not_equal, fill=1.0,
                                                   base=0, pattern=[[-1, D]], channel_multiplier=1), k)
        t_id2 = op(pool, lambda q: q.affine_select(out=ID2[:, :], in_=ID2[:, :], compare_op=ALU.not_equal, fill=1.0,
                                                   base=-D, pattern=[[-1, D]], channel_multiplier=1), t_id2)
        t_idh = op(dve, lambda q: q.tensor_copy(IDH[:, :], IDF[:, :]), t_idf)
        t_qb = [op(dve, lambda q: q.memset(QB[:, :, :], 0.0))]
        t_kb = op(dve, lambda q: q.memset(KB[:, :, :], 0.0))
        t_kb = [op(dve, lambda q: q.memset(KB[:, :, 54:55], 1.0), t_kb)]
        t_kz = [op(pool, lambda q, i=i: q.memset(KZ[i][:, :, :, :], 0.0)) for i in range(2)]
        t_vb = [op(dve, lambda q, i=i: q.memset(VB[i][:, :, :, 18:19], 1.0)) for i in range(2)]

        x_v = I["x"].rearrange("(t p) c -> p t c", p=128)
        t_c = d_c.go(sp, CT[:, :, :], I["cT"].rearrange("(k p) b -> p k b", p=96))
        for q4 in range(4):
            t_x = d_in.go(act, X[:, 4 * q4:4 * q4 + 4, :], x_v[:, 4 * q4:4 * q4 + 4, :])
        for t in range(NT):
            XW[t] = [t_x]
        t_cs = op(act, lambda q: q.activation(CS[:, :, :], CT[:, :, :], ACT.Silu), t_c)

        def cond_rows(w, bias, n, dst, first):
            w_v = w.rearrange("(k p) n -> p k n", p=96)
            toks = []
            for k in range(n // C):
                i, _, free = rSTG.take()
                W = STG[i][0:96, 0:3 * C].rearrange("p (k n) -> p k n", k=3)
                Bb = STG[i][0:B, 3 * C:4 * C]
                d_stg[i].go(sp, W, w_v[:, :, k * C:(k + 1) * C], free)
                t = d_stg[i].go(sp, Bb, bias[k * C:(k + 1) * C].partition_broadcast(B))
                yield
                j, ps, pf = rC.take()
                m = mms([(ps[0:B, 0:C], CS[:, q, :], W[:, q, :]) for q in range(3)], t, t_cs, pf)
                o, _, of = rOS.take()
                a = op(dve, lambda q, o=o, ps=ps, Bb=Bb, f=first(k): q.scalar_tensor_tensor(
                    out=OS[o][:, :], in0=ps[0:B, 0:C], scalar=f, in1=Bb, op0=ALU.add, op1=ALU.add), m, t, of)
                rC.free[j], rSTG.free[i] = [a], [m, a]
                s = d_os[o].go(sp, dst[:, k * C:(k + 1) * C], OS[o][:, :], a)
                rOS.free[o] = [s]
                toks = [x for x in toks if x[0] is not s[0]] + [s]
                yield
            cond_done.append(toks)

        cond_done = []

        def split_cols(dst, src_parts, w, cols, scales):
            done = []
            for blk in range(3):
                i, _, free = rSTG.take()
                S = STG[i]
                if blk < 2:
                    t = d_stg[i].go(sp, S[:, 0:cols], w[blk * 128:(blk + 1) * 128, :], free)
                else:
                    for g in range(4):
                        t = d_stg[i].go(sp, S[32 * g:32 * g + 32, 0:cols], w[256:288, :], free if g == 0 else [])
                yield
                fin = []
                for a, b, s in scales:
                    if blk < 2:
                        h, l = dst[:, blk, a:b], dst[:, 3 + blk, a:b]
                        x = op(act, lambda q, h=h, v=S[:, a:b], s=s: q.activation(h, v, ACT.Copy, scale=s), t, src_parts)
                        y = op(dve, lambda q, h=h, l=l, v=S[:, a:b], s=s: q.scalar_tensor_tensor(
                            out=l, in0=v, scalar=s, in1=h, op0=ALU.mult, op1=ALU.subtract), x, t, src_parts)
                    else:
                        h, l = dst[:, 2, a:b], dst[64:128, 2, a:b]
                        x = op(act, lambda q, h=h, v=S[:, a:b], s=s: q.activation(h, v, ACT.Copy, scale=s), t, src_parts)
                        y = op(dve, lambda q, l=l, v=S[64:128, a:b], s=s: q.scalar_tensor_tensor(
                            out=l, in0=v, scalar=s, in1=l, op0=ALU.mult, op1=ALU.subtract), x, t, src_parts)
                    fin += [x, y]
                rSTG.free[i] = fin
                done += fin
                yield
            tok["split"] = done

        LW = [dict(q=("L0_w_qkv", "L0_b_qkv"), p=("L0_w_proj", "L0_b_proj"), a=("L0_w_adaln", "L0_b_adaln"), ne=4,
                   act=ACT.Gelu_apprx_tanh),
              dict(q=("L1_qkv_w", "L1_qkv_b"), p=("L1_proj_w", "L1_proj_b"), a=("L1_ada_w", "L1_ada_b"), ne=1,
                   act=ACT.Gelu),
              dict(q=("L2_W_qkv", "L2_b_qkv"), p=("L2_W_proj", "L2_b_proj"), a=("L2_W_ada", "L2_b_ada"), ne=1,
                   act=ACT.Gelu_apprx_tanh)]

        def mlp_w(L, e):
            if L == 0:
                return I["L0_w1"][e], I["L0_w2"][e], I["L0_b1T"][:, e, :], I["L0_b2"][e]
            n = ("L1_fc1_w", "L1_fc2_w", "L1_b1T", "L1_fc2_b") if L == 1 else ("L2_W_fc1", "L2_W_fc2", "L2_b1T", "L2_b_fc2")
            return I[n[0]], I[n[1]], I[n[2]], I[n[3]]

        tok = {}
        wq_rd, wp_rd, bias_rd, w2_rd = [[]], [[]], [[]], [[]]
        w1_rd = [[], []]
        w1_at = [0]

        def attn_weights(L):
            w, b = LW[L]["q"]
            d_bias.go(sp, BQ[:, :], I[b].partition_broadcast(128), bias_rd[0])
            t = d_bias.go(sp, BP[:, :], I[LW[L]["p"][1]].partition_broadcast(128))
            t2 = op(dve, lambda q: q.tensor_scalar(BQ[:, 0:C], BQ[:, 0:C], QS, None, ALU.mult), t)
            tok["bias", L] = [t, t2]
            yield from split_cols(WQ, wq_rd[0], I[w], 3 * C, [(0, C, WS * QS), (C, 3 * C, WS)])
            tok["wq", L] = tok["split"]
            yield from split_cols(WP, wp_rd[0], I[LW[L]["p"][0]], C, [(0, C, WS)])
            tok["wp", L] = tok["split"]
            if L == 0:
                yield from split_cols(WG, [], I["L0_w_gate"], NE, [(0, NE, WS)])
                tok["wg"] = tok["split"]

        def mlp_bias(L):
            for e in range(LW[L]["ne"]):
                _, _, b1, b2 = mlp_w(L, e)
                d_bias.go(sp, B1[:, e, :], b1, tok.get("b_rd", []) if e == 0 else [])
                t = d_bias.go(sp, B2[:, e, :], b2.partition_broadcast(128))
            tok["b2", L] = [t]
            yield

        def w1_load(L, e):
            k = w1_at[0] % 2
            w1_at[0] += 1
            yield from split_cols(W1[k], w1_rd[k], mlp_w(L, e)[0], HID, [(0, HID, WS)])
            tok["w1", L, e] = (k, tok["split"])

        def w2_load(L, e):
            w = mlp_w(L, e)[1].rearrange("(m p) n -> p m n", p=128)
            done = []
            for c in range(3):
                i, _, free = rSTG.take()
                S = STG[i][:, 0:3 * C].rearrange("p (m n) -> p m n", m=3)
                t = d_stg[i].go(sp, S, w[:, 3 * c:3 * c + 3, :], free)
                yield
                h, l = W2[:, 3 * c:3 * c + 3, 0, :], W2[:, 3 * c:3 * c + 3, 1, :]
                x = op(act, lambda q, h=h, S=S: q.activation(h, S, ACT.Copy, scale=WS), t, w2_rd[0])
                y = op(dve, lambda q, h=h, l=l, S=S: q.scalar_tensor_tensor(
                    out=l, in0=S, scalar=WS, in1=h, op0=ALU.mult, op1=ALU.subtract), x, t, w2_rd[0])
                rSTG.free[i] = [x, y]
                done += [x, y]
                yield
            tok["w2", L, e] = done

        def to_columns(w, b, y, ytok):
            i, xb, free = rXB[w].take()
            a1 = op(act, lambda q: q.activation(xb[:, :, 0:C], y, ACT.Copy), ytok, free)
            a2 = op(act, lambda q: q.activation(xb[:, :, 320:352], y[:, :, 256:C], ACT.Copy), ytok)
            d1 = op(dve, lambda q: q.tensor_tensor(xb[:, :, 384:640], y[:, :, 0:256], xb[:, :, 0:256], ALU.subtract), a1, ytok, free)
            l2 = xb[:, :, 288:384].rearrange("p t (r c) -> p t r c", c=32)[:, :, 0:3:2, :]
            y2 = y[:, :, 256:C].unsqueeze(2).broadcast_to([128, 2, 2, 32])
            h2 = xb[:, :, 256:288].unsqueeze(2).broadcast_to([128, 2, 2, 32])
            p1 = op(pool, lambda q: q.tensor_tensor(l2, y2, h2, ALU.subtract), a1, ytok, free)
            yield
            toks = []
            for n in range(2):
                t = 2 * b + n
                j, ps, pf = rC.take()
                psh = ps.bitcast(F16)
                for k in range(5):
                    fn = lambda q, psh=psh, k=k, n=n: q.transpose(psh[:, k * 128:(k + 1) * 128], xb[:, n, k * 128:(k + 1) * 128], IDH[:, :])
                    if k < 4:
                        quiet(pe, fn, [a1, a2, d1, p1, pf, t_idh] if k == 0 else [])
                    else:
                        m = op(pe, fn)
                dst = XT[:, :, t * 128:(t + 1) * 128]
                src = psh[:, 0:640].rearrange("p (k t) -> p k t", k=5)
                if n == 0:
                    v = op(act, lambda q, dst=dst, src=src: q.activation(dst, src, ACT.Copy), m, TR[t])
                else:
                    v = op(dve, lambda q, dst=dst, src=src: q.tensor_copy(dst, src), m, TR[t])
                rC.free[j] = [v]
                TW[t], TR[t] = [v], []
                toks.append(m)
                yield
            rXB[w].free[i] = toks
            tok["read"] = [a1, a2, d1, p1]

        def products(ps, lhs, rhs, swap=False):
            return [(ps, lhs(x), rhs(w)) if not swap else (ps, lhs(w), rhs(x)) for x, w in PRODUCTS]

        def layernorm(w, b, sc, sh, adt):
            i, yl, free = rYL[w].take()
            ST, MV, RS = STS[w], MVS[w], RSS[w]
            ts = []
            for n in range(2):
                t = 2 * b + n
                s = op(dve, lambda q, n=n, t=t: q.bn_stats(ST[:, n, :], X[:, t, :]), XW[t], tok.get(("st", w)))
                s = op(dve, lambda q, n=n: q.bn_aggr(MV[:, n, :], ST[:, n, :]), s, tok.get(("mv", w)))
                ts.append(s)
            tok["st", w] = ts
            p = op(pool, lambda q: q.tensor_scalar(RS[:, 0, :], MV[:, :, 1], EPS, None, ALU.add), ts, tok.get(("mv", w)))
            p = op(pool, lambda q: q.tensor_tensor(RS[:, 1, :], RS[:, 0, :], PH[:, :], ALU.pow), p)
            yield
            r = []
            for n in range(2):
                t = 2 * b + n
                y = yl[:, n, :]
                a = op(dve, lambda q, n=n, t=t, y=y: q.scalar_tensor_tensor(
                    out=y, in0=X[:, t, :], scalar=MV[:, n, 0:1], in1=sc, op0=ALU.subtract, op1=ALU.mult), ts, adt, XW[t], free)
                XR[t] = XR[t] + [a]
                r.append(a)
            for n in range(2):
                y = yl[:, n, :]
                r[n] = op(dve, lambda q, n=n, y=y: q.scalar_tensor_tensor(
                    out=y, in0=y, scalar=RS[:, 1, n:n + 1], in1=sh, op0=ALU.mult, op1=ALU.add), r[n], p)
            tok["mv", w] = r
            yield
            yield from to_columns(w, b, yl, r)
            rYL[w].free[i] = tok["read"]
            tok["lnd"] = r

        qt_rd, kz_rd, vb_rd = [[], []], [[], []], [[], []]
        qb_rd, kb_rd, nm_rd, mt_rd = [[]], [[]], [[]], [[]]
        ad_rd, ae_rd = [[], []], [[], []]

        def prep(L, b):
            u = b % 2
            adt = d_ad[u].go(sp, AD1[u], scr_ada[L, b, 0:2 * C].partition_broadcast(128), ad_rd[u], tok["ada", L])
            yield
            yield from layernorm(0, b, AD1[u][:, C:2 * C], AD1[u][:, 0:C], adt)
            ad_rd[u] = [tok["lnd"]]
            wr_q, wr_k, wr_v = [], [], []
            for n in range(2):
                t = 2 * b + n
                iy, y, yf = rY.take()
                ev = []
                for half in range(2):
                    j, ps, pf = rC.take()
                    o = ps[:, 0:432]
                    m = mms(products(o, lambda x: XT[:, x, t * 128:(t + 1) * 128],
                                     lambda w: WQ[:, w, half * 432:(half + 1) * 432]), TW[t], tok["wq", L], pf)
                    dst = y[:, half * 432:(half + 1) * 432]
                    bq = BQ[:, half * 432:(half + 1) * 432]
                    v = op(dve, lambda q, o=o, dst=dst, bq=bq: q.scalar_tensor_tensor(
                        out=dst, in0=o, scalar=1.0 / WS, in1=bq, op0=ALU.mult, op1=ALU.add), m, tok["bias", L], yf)
                    rC.free[j] = [v]
                    ev.append(v)
                    yield
                TR[t] = [m]
                wq_rd[0] = [m]
                bias_rd[0] = [v]
                yq, yk, yv = (y[:, s * C:(s + 1) * C].rearrange("p (h d) -> p h d", d=HD) for s in range(3))
                if L == 1:
                    yield from heads(b, n, yq, yk, yv, ev)
                    rY.free[iy] = tok["hd"]
                    continue
                yq2, yk2 = (z.unsqueeze(2).broadcast_to([128, NH, 2, HD]) for z in (yq, yk))
                qh = QB[:, :, 0:54].rearrange("p h (r d) -> p h r d", d=HD)[:, :, 0:3:2, :]
                kh = KB[:, :, 0:36].rearrange("p h (r d) -> p h r d", d=HD)
                a1 = op(act, lambda q, qh=qh, v=yq2: q.activation(qh, v, ACT.Copy), ev, qb_rd[0], t_qb)
                a2 = op(act, lambda q, kh=kh, v=yk2: q.activation(kh, v, ACT.Copy), ev, kb_rd[0], t_kb)
                vh, vl = VB[u][:, n, :, 0:18], VB[u][:, n, :, 19:37]
                a3 = op(act, lambda q, vh=vh, v=yv: q.activation(vh, v, ACT.Copy), ev, vb_rd[u], t_vb)
                d1 = op(dve, lambda q, v=yq: q.tensor_tensor(QB[:, :, 18:36], v, QB[:, :, 0:18], ALU.subtract), a1, ev, qb_rd[0], t_qb)
                p1 = op(pool, lambda q, v=yk: q.tensor_tensor(KB[:, :, 36:54], v, KB[:, :, 0:18], ALU.subtract), a2, ev, kb_rd[0], t_kb)
                d3 = op(dve, lambda q, v=yv, vh=vh, vl=vl: q.tensor_tensor(vl, v, vh, ALU.subtract), a3, ev, vb_rd[u])
                rY.free[iy] = [a1, a2, a3, d1, p1, d3]
                wr_v += [a3, d3]
                yield
                for src, deps, rd in ((QB, [a1, d1, t_qb], qb_rd), (KB, [a2, p1, t_kb], kb_rd)):
                    j, ps, pf = rC.take()
                    psh = ps.bitcast(F16)
                    for c in range(8):
                        fn = lambda q, psh=psh, c=c, src=src: q.transpose(
                            psh[:, c * 128:(c + 1) * 128], src[:, 2 * c:2 * c + 2, :].rearrange("p a b -> p (a b)"), IDH[:, :])
                        if c < 7:
                            quiet(pe, fn, [deps, pf, t_idh] if c == 0 else [])
                        else:
                            m = op(pe, fn)
                    rd[0] = [m]
                    s3 = psh.rearrange("p (c t) -> p c t", c=8)
                    if src is QB:
                        v = op(dve, lambda q, s3=s3, n=n: q.tensor_copy(QT[u][:, :, n * 128:(n + 1) * 128], s3), m, qt_rd[u])
                        wr_q.append(v)
                        rC.free[j] = [v]
                    else:
                        v1 = op(act, lambda q, s3=s3, n=n: q.activation(KZ[u][0:64, :, 0, n * 128:(n + 1) * 128], s3[0:64], ACT.Copy), m, kz_rd[u], t_kz)
                        v2 = op(dve, lambda q, s3=s3, n=n: q.tensor_copy(KZ[u][64:128, :, 1, n * 128:(n + 1) * 128], s3[64:128]), m, kz_rd[u], t_kz)
                        wr_k += [v1, v2]
                        rC.free[j] = [v1, v2]
                    yield
            if L == 1:
                return
            tok["v", b] = wr_v
            mx = []
            for c in range(8):
                for n in range(2):
                    j, ps, pf = rC.take()
                    m = mms([(ps, QT[u][:, c, n * 128:(n + 1) * 128], KZ[u][:, c, :, :].rearrange("p a b -> p (a b)"))],
                            wr_q, wr_k, pf, t_kz)
                    v = op(dve, lambda q, ps=ps, n=n, c=c: q.tensor_reduce(
                        NM[:, n, :, c], ps.rearrange("p (a k) -> p a k", a=2), AX.X, ALU.max, negate=True), m, nm_rd[0])
                    rC.free[j] = [v]
                    mx.append(v)
                yield
            j, ps, pf = rC.take()
            psh = ps.bitcast(F16)
            for n in range(2):
                m = op(pe, lambda q, psh=psh, n=n: q.transpose(
                    psh[0:16, n * 128:(n + 1) * 128], NM[:, n, :, :].rearrange("p a b -> p (a b)"), IDH[:, :]), mx, pf, t_idh)
            nm_rd[0] = [m]
            v = op(act, lambda q, psh=psh: q.activation(MT[:, :], psh[0:16, 0:256], ACT.Copy), m, mt_rd[0])
            rC.free[j] = [v]
            d_mt[u].go(sp, QT[u][54:55, :, :], MT[0:8, :], v, m)
            t2 = d_mt[u].go(sp, QT[u][118:119, :, :], MT[8:16, :])
            mt_rd[0] = [t2]
            tok["qk", b] = [wr_q, wr_k, t2]
            yield

        on_rd, dn_rd, yo_rd = [[]], [[]], [[]]
        hs_free = {"s": [], "o": [[], []]}

        def heads(b, n, yq, yk, yv, ev):
            dv, rd = [], []
            for c in range(4):
                i, big, bf = rHB.take()
                t3 = big.rearrange("p (h k d) -> p h k d", h=4, d=HD)
                a = yq[:, 4 * c:4 * c + 4, :].unsqueeze(2).broadcast_to([128, 4, NH, HD])
                k = yk.unsqueeze(1).broadcast_to([128, 4, NH, HD])
                e = pool if c % 2 else dve
                m = op(e, lambda q, t3=t3, a=a, k=k: q.tensor_tensor(t3, a, k, ALU.mult), ev, bf)
                rd.append(m)
                v = op(dve, lambda q, t3=t3, c=c: q.tensor_reduce(SC[:, 4 * c:4 * c + 4, :], t3, AX.X, ALU.add), m, hs_free["s"])
                rHB.free[i] = [v]
                dv.append(v)
                yield
            r = op(dve, lambda q: q.tensor_reduce(SM[:, 0:NH], SC, AX.X, ALU.max), dv)
            r = op(dve, lambda q: q.tensor_tensor(SC, SC, SM[:, 0:NH].unsqueeze(2).broadcast_to([128, NH, NH]), ALU.subtract), r)
            x = op(act, lambda q: q.activation(SC, SC, ACT.Exp), r)
            r = op(dve, lambda q: q.tensor_reduce(SM[:, 0:NH], SC, AX.X, ALU.add), x)
            r = op(dve, lambda q: q.reciprocal(SM[:, NH:2 * NH], SM[:, 0:NH]), r)
            yield
            o = ON[:, :, :, :].rearrange("p a b c -> p (a b c)")[:, n * C:(n + 1) * C].rearrange("p (h d) -> p h d", d=HD)
            ov, mu = [], []
            for c in range(4):
                i, big, bf = rHB.take()
                t3 = big.rearrange("p (h d k) -> p h d k", h=4, d=HD)
                a = SC[:, 4 * c:4 * c + 4, :].unsqueeze(2).broadcast_to([128, 4, HD, NH])
                k = yv.rearrange("p k d -> p d k").unsqueeze(1).broadcast_to([128, 4, HD, NH])
                e = pool if c % 2 else dve
                m = op(e, lambda q, t3=t3, a=a, k=k: q.tensor_tensor(t3, a, k, ALU.mult), x, ev, bf)
                mu.append(m)
                v = op(dve, lambda q, t3=t3, o=o, c=c: q.tensor_reduce(o[:, 4 * c:4 * c + 4, :], t3, AX.X, ALU.add), m, hs_free["o"][n])
                rHB.free[i] = [v]
                ov.append(v)
                yield
            v = op(dve, lambda q, o=o: q.tensor_tensor(o, o, SM[:, NH:2 * NH].unsqueeze(2).broadcast_to([128, NH, HD]), ALU.mult), ov, r)
            hs_free["s"] = [v, mu]
            t = d_ho[n].go(sp, scr_o[b, :, n * 128:(n + 1) * 128, :].rearrange("h t d -> t h d"), o, v)
            hs_free["o"][n] = [t]
            tok["ho", b, n] = t
            tok["hd"] = [rd, mu]
            yield

        def regroup(L, b):
            u = b % 2
            tok["ad", b] = d_ae[u].go(sp, AD2[u], scr_ada[L, b, 2 * C:5 * C].partition_broadcast(128), ae_rd[u], tok["ada", L])
            src = scr_o[b].rearrange("h t d -> (h t d)").rearrange("(n p c) -> p n c", p=128, c=C)
            tok["o", b] = [d_yo.go(sp, YO, src, yo_rd[0], tok["ho", b, 0], tok["ho", b, 1])]
            yield

        def attend(L, b):
            u = b % 2
            tok["ad", b] = d_ae[u].go(sp, AD2[u], scr_ada[L, b, 2 * C:5 * C].partition_broadcast(128), ae_rd[u], tok["ada", L])
            pend = []
            og = {}
            red, rec = [], []

            def av(c, s, ready):
                if c % 2 == 0:
                    og["s"] = rO.take()
                j, ps, pf = og["s"]
                for par in range(2):
                    h = 2 * c + par
                    for n in range(2):
                        at = (n * 4 + (h % 4)) * 37
                        big, small = ps[:, at:at + 37], ps[:, at:at + 19]
                        items = [(big, PHI[s][:, kt, par, n * 128:(n + 1) * 128], VB[u][:, kt, h, :]) for kt in range(2)]
                        items += [(small, PLO[s][:, kt, par, n * 128:(n + 1) * 128], VB[u][:, kt, h, 0:19]) for kt in range(2)]
                        m = mms(items, ready, pf, tok["v", b], t_vb)
                rE.free[s] = [m] + [ready]
                if c % 2 == 1:
                    g = c // 2
                    o8 = ps[:, 0:296].rearrange("p (g x) -> p g x", x=37)
                    r = op(dve, lambda q, o8=o8, g=g: q.reciprocal(DN[:, g, :], o8[:, :, 18]), m, dn_rd[0])
                    pair = bass.AP(ps.tensor, ps.offset, [list(ps.ap[0]), [37, 8], [1, 18], [19, 2]])
                    v = op(dve, lambda q, pair=pair, g=g: q.tensor_reduce(
                        ON[:, g, :, :].rearrange("p n (h d) -> p (n h) d", d=HD), pair, AX.X, ALU.add), m, on_rd[0])
                    rO.free[j] = [r, v]
                    red.append(v)
                    rec.append(r)
                return m

            for c in range(8):
                i, ps, pf = rA.take()
                p4 = ps.rearrange("p (k a t) -> p k a t", k=2, a=2)
                for kt in range(2):
                    for par in range(2):
                        m = mms([(p4[:, kt, par, :], KZ[u][:, c, par, kt * 128:(kt + 1) * 128], QT[u][:, c, :])],
                                tok["qk", b], pf, t_kz)
                s, _, ef = rE.take()
                a1 = op(act, lambda q, ps=ps, s=s: q.activation(E32[s], ps, ACT.Exp), m, ef)
                hi = PHI[s].rearrange("p k a t -> p (k a t)")
                lo = PLO[s].rearrange("p k a t -> p (k a t)")
                a2 = op(act, lambda q, ps=ps, hi=hi: q.activation(hi, ps, ACT.Exp), m, ef)
                rA.free[i] = [a1, a2]
                yield
                z = 640
                d = op(dve, lambda q, s=s, hi=hi, lo=lo: q.tensor_tensor(lo[:, 0:z], E32[s][:, 0:z], hi[:, 0:z], ALU.subtract), a1, a2, ef)
                p = op(pool, lambda q, s=s, hi=hi, lo=lo: q.tensor_tensor(lo[:, z:1024], E32[s][:, z:1024], hi[:, z:1024], ALU.subtract), a1, a2, ef)
                pend.append((c, s, [a2, d, p]))
                if len(pend) > 1:
                    m2 = av(*pend.pop(0))
                yield
            m2 = av(*pend.pop(0))
            qt_rd[u], kz_rd[u], vb_rd[u] = [m], [m], [m2]
            yield
            outs = []
            for n in range(2):
                o3 = YO[:, n, :].rearrange("p (g h d) -> p g h d", g=4, d=HD)
                i3 = ON[:, :, n, :].rearrange("p g (h d) -> p g h d", d=HD)
                r3 = DN[:, :, n * 4:n * 4 + 4].unsqueeze(3).broadcast_to([128, 4, 4, HD])
                outs.append(op(dve, lambda q, o3=o3, i3=i3, r3=r3: q.tensor_tensor(o3, i3, r3, ALU.mult), red, rec, yo_rd[0]))
            on_rd[0] = dn_rd[0] = outs
            tok["o", b] = outs
            yield

        gb_rd = [[]]

        def finish(L, b):
            u = b % 2
            g1 = AD2[u][:, 0:C]
            adt = tok["ad", b]
            p = op(pool, lambda q: q.tensor_tensor(GB[:, :], g1, BP[:, :], ALU.mult), adt, tok["bias", L], gb_rd[0])
            pb = []
            for n in range(2):
                t = 2 * b + n
                pb.append(op(pool, lambda q, t=t: q.tensor_tensor(X[:, t, :], X[:, t, :], GB[:, :], ALU.add), p, XW[t], XR[t]))
                XW[t], XR[t] = [pb[n]], []
            gb_rd[0] = pb
            yield from to_columns(1, b, YO, tok["o", b])
            yo_rd[0] = tok["read"]
            for n in range(2):
                t = 2 * b + n
                j, ps, pf = rC.take()
                o = ps[:, 0:C]
                m = mms(products(o, lambda x: XT[:, x, t * 128:(t + 1) * 128], lambda w: WP[:, w, :]), TW[t], tok["wp", L], pf)
                TR[t] = [m]
                wp_rd[0] = [m]
                k, tm, tf = rTM.take()
                v = op(dve, lambda q, o=o, tm=tm: q.scalar_tensor_tensor(
                    out=tm, in0=o, scalar=1.0 / WS, in1=g1, op0=ALU.mult, op1=ALU.mult), m, adt, tf)
                rC.free[j] = [v]
                v = op(dve, lambda q, t=t, tm=tm: q.tensor_tensor(X[:, t, :], X[:, t, :], tm, ALU.add), v, XW[t])
                rTM.free[k] = [v]
                XW[t] = [v]
                yield
            yield from layernorm(1, b, AD2[u][:, 2 * C:3 * C], AD2[u][:, C:2 * C], adt)
            ae_rd[u] = [tok["lnd"], p, v]
            bias_rd[0] = [bias_rd[0], p]
            if L == 0:
                for n in range(2):
                    t = 2 * b + n
                    j, ps, pf = rC.take()
                    o = ps[:, 0:NE]
                    m = mms(products(o, lambda x: XT[:, x, t * 128:(t + 1) * 128], lambda w: WG[:, w, :]), TW[t], tok["wg"], pf)
                    v = op(dve, lambda q, o=o, t=t: q.tensor_scalar(LG[:, t, :], o, 1.0 / WS, None, ALU.mult), m)
                    rC.free[j] = [v]
                    tok["lg", t] = v
                yield

        def gates():
            lg = [tok["lg", t] for t in range(NT)]
            l3 = LG[:, :, :]
            a = op(dve, lambda q: q.tensor_reduce(L1[:, :], l3, AX.X, ALU.max), lg)
            b = op(dve, lambda q: q.tensor_tensor(CW[:, :, :], l3, L1[:, :].unsqueeze(2).broadcast_to([128, NT, NE]), ALU.subtract), a)
            c = op(act, lambda q: q.activation(CW[:, :, :], CW[:, :, :], ACT.Exp), b)
            e4 = l3.unsqueeze(3).broadcast_to([128, NT, NE, NE])
            j4 = l3.unsqueeze(2).broadcast_to([128, NT, NE, NE])
            t4 = LT[:, :, :].rearrange("p t (e j) -> p t e j", e=NE)
            m4 = LM[:, :, :].rearrange("p t (e j) -> p t e j", e=NE)
            d = op(dve, lambda q: q.tensor_tensor(t4, j4, e4, ALU.is_gt), lg)
            e = op(dve, lambda q: q.tensor_tensor(m4, j4, e4, ALU.is_equal), lg)
            e = op(dve, lambda q: q.tensor_tensor(LM[:, :, :], LM[:, :, :], TRI[:, :].unsqueeze(1).broadcast_to([128, NT, 16]), ALU.mult), e, t_tri)
            e = op(dve, lambda q: q.tensor_tensor(LT[:, :, :], LT[:, :, :], LM[:, :, :], ALU.add), e, d)
            e = op(dve, lambda q: q.tensor_reduce(CWS[:, :, :], t4, AX.X, ALU.add), e)
            e = op(dve, lambda q: q.tensor_scalar(CWS[:, :, :], CWS[:, :, :], 1.5, None, ALU.is_lt), e)
            f = op(dve, lambda q: q.tensor_tensor(CW[:, :, :], CW[:, :, :], CWS[:, :, :], ALU.mult), e, c)
            g = op(dve, lambda q: q.tensor_reduce(L1[:, :], CW[:, :, :], AX.X, ALU.add), f)
            g = op(dve, lambda q: q.reciprocal(L1[:, :], L1[:, :]), g)
            g = op(dve, lambda q: q.tensor_tensor(CW[:, :, :], CW[:, :, :], L1[:, :].unsqueeze(2).broadcast_to([128, NT, NE]), ALU.mult), g, f)
            h = op(dve, lambda q: q.tensor_scalar(CWS[:, :, :], CW[:, :, :], 1.0 / WS, None, ALU.mult), g)
            tok["cw"] = [g, h]

        G2 = ADB[:, 0:B * C].rearrange("p (b c) -> p b c", c=C)
        nh = [0]

        def mlp(L, fence):
            fn_act = LW[L]["act"]
            ne = LW[L]["ne"]
            g2t = d_g2.go(sp, G2, scr_ada[L, :, 5 * C:6 * C].partition_broadcast(128), ad_rd, ae_rd, fence)
            hw = {}
            hfree = [[fence], [fence]]

            def up(e, c):
                k, wt = tok["w1", L, e]
                u = nh[0] % 2
                nh[0] += 1
                done = []
                xt = [TW[t] for t in range(4 * c, 4 * c + 4)]
                for m in range(9):
                    i, ps, pf = rA4.take()
                    mt = mms(products(ps, lambda w: W1[k][:, w, m * 128:(m + 1) * 128],
                                      lambda x: XT[:, x, c * 512:(c + 1) * 512], swap=True), wt, xt, pf)
                    gi, g, gf = rG.take()
                    bias = B1[:, e, m:m + 1]
                    hi, lo = Hh[u][:, m, 0, :], Hh[u][:, m, 1, :]
                    a1 = op(act, lambda q, g=g, ps=ps, bias=bias: q.activation(g, ps, fn_act, scale=1.0 / WS, bias=bias), mt, gf, tok["b2", L])
                    a2 = op(act, lambda q, hi=hi, ps=ps, bias=bias: q.activation(hi, ps, fn_act, scale=1.0 / WS, bias=bias), mt, hfree[u])
                    d = op(dve, lambda q, g=g, hi=hi, lo=lo: q.tensor_tensor(lo, g, hi, ALU.subtract), a1, a2, hfree[u])
                    rA4.free[i] = [a1, a2]
                    rG.free[gi] = [d]
                    done += [a2, d]
                    yield
                w1_rd[k] = [mt]
                for t in range(4 * c, 4 * c + 4):
                    TR[t] = TR[t] + [mt]
                hw[e, c] = (u, done[-2:])

            def down(e, c):
                u, ht = hw[e, c]
                for n in range(4):
                    t = 4 * c + n
                    i, ps, pf = rF.take()
                    o = ps[:, 0:C]
                    items = []
                    for m in range(9):
                        hi, lo = (Hh[u][:, m, s, n * 128:(n + 1) * 128] for s in range(2))
                        items += [(o, hi, W2[:, m, 0, :]), (o, hi, W2[:, m, 1, :]), (o, lo, W2[:, m, 0, :])]
                    mt = mms(items, ht, tok["w2", L, e], pf)
                    k, tm, tf = rTM.take()
                    scal = CWS[:, t, e:e + 1] if L == 0 else 1.0 / WS
                    g = G2[:, t // 2, :]
                    v = op(dve, lambda q, o=o, tm=tm, scal=scal, g=g: q.scalar_tensor_tensor(
                        out=tm, in0=o, scalar=scal, in1=g, op0=ALU.mult, op1=ALU.mult), mt, g2t, tf, tok.get("cw") if L == 0 else [])
                    rF.free[i] = [v]
                    v2 = op(pool, lambda q, t=t, tm=tm: q.tensor_tensor(X[:, t, :], X[:, t, :], tm, ALU.add), v, XW[t], XR[t])
                    rTM.free[k] = [v2]
                    XW[t], XR[t] = [v2], []
                    yield
                hfree[u] = [mt]
                w2_rd[0] = [mt]
                tok["g2rd"] = [v]

            def bias_rows():
                for t in range(NT):
                    if L == 0:
                        k, tm, tf = rTM.take()
                        v = op(dve, lambda q, t=t, tm=tm: q.tensor_scalar(tm, B2[:, 0, :], CW[:, t, 0:1], None, ALU.mult), tf, tok["b2", L], tok["cw"])
                        for e in range(1, NE):
                            v = op(dve, lambda q, t=t, tm=tm, e=e: q.scalar_tensor_tensor(
                                out=tm, in0=B2[:, e, :], scalar=CW[:, t, e:e + 1], in1=tm, op0=ALU.mult, op1=ALU.add), v)
                        v = op(pool, lambda q, t=t, tm=tm: q.tensor_tensor(tm, tm, G2[:, t // 2, :], ALU.mult), v, g2t)
                        v = op(pool, lambda q, t=t, tm=tm: q.tensor_tensor(X[:, t, :], X[:, t, :], tm, ALU.add), v, XW[t], XR[t])
                        rTM.free[k] = [v]
                    else:
                        v = op(pool, lambda q, t=t: q.tensor_tensor(GB[:, :], G2[:, t // 2, :], B2[:, 0, :], ALU.mult), g2t, tok["b2", L], gb_rd[0])
                        v = op(pool, lambda q, t=t: q.tensor_tensor(X[:, t, :], X[:, t, :], GB[:, :], ALU.add), v, XW[t], XR[t])
                        gb_rd[0] = [v]
                    XW[t], XR[t] = [v], []
                    yield

            seq = [(e, c) for e in range(ne) for c in range(4)]
            br = bias_rows()
            yield from up(*seq[0])
            for k, (e, c) in enumerate(seq):
                wl = None
                if c == 0 and e + 1 < ne:
                    wl = w1_load(L, e + 1)
                nxt = up(*seq[k + 1]) if k + 1 < len(seq) else iter(())
                sides = [(br, 1.0)]
                if wl is not None:
                    sides.append((wl, 1.0))
                yield from steps(nxt, *sides)
                if c == 0 and e > 0:
                    run(w2_load(L, e))
                yield from steps(down(e, c), (br, 1.0))
            run(br)
            tok["b_rd"] = last()

        def expm_steps():
            run_v = cond_done_v[0]
            z = op(pool, lambda q: q.memset(EX[:, :, :, :], 0.0))
            off = 0
            for i in range(D - 1):
                n = D - 1 - i
                for hf in range(2):
                    dst = EX[64 * hf + i:64 * hf + i + 1, :, 0, i + 1:D]
                    src = scr_v.rearrange("(q h) n -> h q n", h=2)[hf:hf + 1, :, off:off + n]
                    t = d_v.go(sp, dst, src, [z, run_v], allow_slow_non_contiguous=(n == 1))
                off += n
                if i % 8 == 7:
                    yield
            yield

            def pairs(ps, kinds, lhs, rhs, *deps):
                n = 0
                for q4 in range(4):
                    for hf in range(2):
                        sl = slice(64 * hf, 64 * hf + 64)
                        for kd in range(kinds):
                            m = mms([(ps[sl, q4, kd, :], lhs(sl, q4, kd), rhs(sl, q4, kd))], deps)
                return m

            def bank():
                j, ps, pf = rS.take()
                return j, ps.rearrange("p (q k n) -> p q k n", q=4, k=2), pf

            s = 2.0 ** -NSQ
            j, ps, pf = bank()
            m = pairs(ps, 1, lambda sl, a, k: EX[sl, a, 0, :], lambda sl, a, k: ID2[sl, :], t, z, t_id2, pf)
            v = op(dve, lambda q: q.tensor_tensor(EY[:, :, 1, :], ps[:, :, 0, :], EX[:, :, 0, :], ALU.subtract), m, t, z)
            rS.free[j] = [v]
            a = op(dve, lambda q: q.tensor_scalar(EX[:, :, 0, :], EY[:, :, 1, :], -s, None, ALU.mult), v, m)
            a2 = op(dve, lambda q: q.tensor_scalar(EX[:, :, 1, :], EY[:, :, 1, :], s, None, ALU.mult), v, m)
            yield
            j, p1, pf = bank()
            m = pairs(p1, 1, lambda sl, a, k: EX[sl, a, 1, :], lambda sl, a, k: EX[sl, a, 0, :], a, a2, pf)
            y1 = op(dve, lambda q: q.tensor_copy(EY[:, :, 0, :], p1[:, :, 0, :]), m, a, a2)
            rS.free[j] = [y1]
            yield
            j, p2, pf = bank()
            m = pairs(p2, 1, lambda sl, a, k: EY[sl, a, 0, :], lambda sl, a, k: EY[sl, a, 0, :], y1, pf)
            y2 = op(dve, lambda q: q.tensor_copy(EY[:, :, 1, :], p2[:, :, 0, :]), m, y1)
            rS.free[j] = [y2]
            yield
            j, p3, pf = bank()
            m = pairs(p3, 2, lambda sl, a, k: EY[sl, a, 1, :], lambda sl, a, k: EY[sl, a, k, :], y2, y1, pf)
            Cc, Gg, Sx = EW[:, :, 0, :], EW[:, :, 1, :], EW[:, :, 2, :]
            idb = ID2[:, :].unsqueeze(1).broadcast_to([128, 4, D])
            c1 = op(dve, lambda q: q.tensor_scalar(Cc, EY[:, :, 0, :], 0.5, None, ALU.mult), y1)
            g1 = op(dve, lambda q: q.scalar_tensor_tensor(out=Gg, in0=EY[:, :, 0, :], scalar=1.0 / 6, in1=idb, op0=ALU.mult, op1=ALU.add), y1, t_id2)
            for src, fc, fg, dp in ((EY[:, :, 1, :], 1.0 / 24, 1.0 / 120, y2), (p3[:, :, 0, :], 1.0 / 720, 1.0 / 5040, m),
                                    (p3[:, :, 1, :], 1.0 / 40320, 1.0 / 362880, m)):
                c1 = op(dve, lambda q, src=src, fc=fc: q.scalar_tensor_tensor(out=Cc, in0=src, scalar=fc, in1=Cc, op0=ALU.mult, op1=ALU.add), c1, dp)
                g1 = op(dve, lambda q, src=src, fg=fg: q.scalar_tensor_tensor(out=Gg, in0=src, scalar=fg, in1=Gg, op0=ALU.mult, op1=ALU.add), g1, dp)
            rS.free[j] = [c1, g1]
            yield
            j, p5, pf = bank()
            m = pairs(p5, 1, lambda sl, a, k: EX[sl, a, 1, :], lambda sl, a, k: EW[sl, a, 1, :], g1, pf)
            e1 = op(dve, lambda q: q.tensor_tensor(EY[:, :, 0, :], p5[:, :, 0, :], Cc, ALU.add), m, c1)
            e2 = op(dve, lambda q: q.scalar_tensor_tensor(out=EY[:, :, 1, :], in0=p5[:, :, 0, :], scalar=-1.0, in1=Cc, op0=ALU.mult, op1=ALU.add), m, c1)
            rS.free[j] = [e1, e2]
            dn = [e1, e2, m]
            yield
            cur, oth = EY, EX
            for _ in range(NSQ):
                j, p6, pf = bank()
                m = pairs(p6, 2, lambda sl, a, k: cur[sl, a, 1 - k, :], lambda sl, a, k: cur[sl, a, k, :], dn, pf)
                dn = [op(dve, lambda q, o=oth, c=cur, p6=p6: q.scalar_tensor_tensor(
                    out=o[:, :, :, :].rearrange("p a b c -> p (a b c)"), in0=c[:, :, :, :].rearrange("p a b c -> p (a b c)"), scalar=2.0,
                    in1=p6.rearrange("p a b c -> p (a b c)"), op0=ALU.mult, op1=ALU.add), m, dn)]
                rS.free[j] = dn
                dn = dn + [m]
                cur, oth = oth, cur
                yield
            tok["E"] = (cur, dn)

        def householder():
            t = d_p.go(sp, AT[:, :], I["PT"])
            at = [t]
            nb, sg, g, rt, w, d = (HS[:, k:k + 1] for k in range(6))
            hs, n2t = [], []
            hp = sb("HP", [D, 1])
            t_hp = op(pool, lambda q: q.memset(hp[:, :], 0.5))
            sqw = []
            yield
            for j in range(D):
                c, ps, pf = rS.take()
                bc = ps[0:D, 0:C - j]
                aj = AT[:, j:C]
                m = mms([(bc, IDF[0:D, j:j + 1].broadcast_to([D, D]), aj)], at, t_idf, pf)
                s1 = op(act, lambda q, bc=bc, j=j: q.activation(sq[:, j:C], bc, ACT.Square, accum_out=N2[:, 0:1]), m, n2t, sqw)
                s2 = op(dve, lambda q, bc=bc, aj=aj, j=j: q.tensor_tensor_reduce(
                    out=HQ[:, j:C], in0=bc, in1=aj, scale=1.0, scalar=0.0, op0=ALU.mult, op1=ALU.add, accum_out=d), m, s1, at, hs)
                p = op(pool, lambda q: q.tensor_tensor(N2[:, 1:2], N2[:, 0:1], hp[:, :], ALU.pow), s1, t_hp, n2t)
                a = op(dve, lambda q, bc=bc: q.tensor_scalar(sg, bc[:, 0:1], 0.0, 2.0, ALU.is_ge, ALU.mult), m, s1, hs)
                yield
                b = op(dve, lambda q: q.scalar_tensor_tensor(out=nb, in0=sg, scalar=1.0, in1=N2[:, 1:2], op0=ALU.subtract, op1=ALU.mult), a, p, hs)
                e = op(dve, lambda q, bc=bc, j=j: q.scalar_tensor_tensor(out=TI[:, j:j + 1], in0=nb, scalar=bc[:, 0:1], in1=N2[:, 0:1], op0=ALU.mult, op1=ALU.add), b, s1)
                r = op(dve, lambda q, j=j: q.reciprocal(rt, TI[:, j:j + 1]), e, hs)
                f = op(dve, lambda q, j=j: q.scalar_tensor_tensor(out=w, in0=AT[:, j:j + 1], scalar=nb, in1=d, op0=ALU.mult, op1=ALU.add), b, s2, hs, at)
                g1 = op(dve, lambda q, j=j: q.scalar_tensor_tensor(out=g, in0=w, scalar=rt, in1=NMK[:, j:j + 1], op0=ALU.mult, op1=ALU.mult), f, r, t_nmk, hs)
                x = op(dve, lambda q, bc=bc, aj=aj: q.scalar_tensor_tensor(out=aj, in0=bc, scalar=g, in1=aj, op0=ALU.mult, op1=ALU.add), g1, m, s2)
                y = op(dve, lambda q, j=j: q.scalar_tensor_tensor(out=AT[:, j:j + 1], in0=g, scalar=nb, in1=AT[:, j:j + 1], op0=ALU.mult, op1=ALU.add), x)
                y = op(dve, lambda q, j=j: q.scalar_tensor_tensor(out=AT[:, j:j + 1], in0=IDF[0:D, j:j + 1], scalar=nb, in1=AT[:, j:j + 1], op0=ALU.mult, op1=ALU.add), y, t_idf)
                rS.free[c] = [y]
                at = [x, y]
                hs = [y]
                n2t = [y, p]
                sqw = [s1]
                yield
            v0 = op(pool, lambda q: q.memset(UT[0:D, :], 0.0))
            cp = op(dve, lambda q: q.tensor_tensor(UT[0:D, 0:D], AT[:, 0:D], MGE[:, :], ALU.mult), at, v0, t_m)
            cp2 = op(dve, lambda q: q.tensor_copy(UT[0:D, D:C], AT[:, D:C]), at, v0)
            VT = UT[0:D, :]
            vt = [cp, cp2]
            j, ps, pf = rS.take()
            for k in range(3):
                m = op(pe, lambda q, k=k, ps=ps: q.transpose(ps[0:96, k * D:(k + 1) * D], VT[:, k * 96:(k + 1) * 96], IDF[0:D, 0:D]), vt, pf, t_idf)
            VR = STGV[:, 0:3 * D].rearrange("p (k n) -> p k n", k=3)
            c1 = op(dve, lambda q, ps=ps: q.tensor_copy(VR, ps[0:96, 0:3 * D].rearrange("p (k n) -> p k n", k=3)), m, cond_done_v[0])
            rS.free[j] = [c1]
            yield
            j, ps, pf = rS.take()
            m = mms([(ps[0:D, 0:D], VR[:, k, :], VR[:, k, :]) for k in range(3)], c1, pf)
            dg = HS[:, 6:7]
            di = HS[:, 7:8]
            q1 = op(dve, lambda q: q.tensor_tensor_reduce(out=NN[:, 0, :], in0=TI[:, :], in1=IDF[0:D, 0:D], scale=1.0, scalar=0.0,
                                                          op0=ALU.mult, op1=ALU.add, accum_out=dg), at)
            q2 = op(dve, lambda q: q.reciprocal(di, dg), q1)
            q3 = op(dve, lambda q, ps=ps: q.scalar_tensor_tensor(out=NN[:, 0, :], in0=ps[0:D, 0:D], scalar=di, in1=MLT[:, :], op0=ALU.mult, op1=ALU.mult), q2, m)
            rS.free[j] = [q3]
            yield
            j, ps, pf = rS.take()
            m = op(pe, lambda q, ps=ps: q.transpose(ps[0:D, 0:D], NN[:, 0, :], IDF[0:D, 0:D]), q3, pf)
            nt = op(dve, lambda q, ps=ps: q.tensor_copy(NN[:, 1, :], ps[0:D, 0:D]), m)
            pt = op(dve, lambda q, ps=ps: q.scalar_tensor_tensor(out=NP[:, 0, :], in0=ps[0:D, 0:D], scalar=-1.0, in1=IDF[0:D, 0:D], op0=ALU.mult, op1=ALU.add), m)
            rS.free[j] = [nt, pt]
            cur = 0
            nn = [q3, nt]
            prd = []
            yield
            for k in range(5):
                j, ps, pf = rS.take()
                m1 = mms([(ps[0:D, 0:D], NN[:, 2 * cur + 1, :], NN[:, 2 * cur, :])], nn, pf)
                m1 = mms([(ps[0:D, D:2 * D], NN[:, 2 * cur, :], NN[:, 2 * cur + 1, :])])
                nx = 1 - cur
                c2 = op(dve, lambda q, ps=ps, nx=nx: q.tensor_copy(NN[:, 2 * nx:2 * nx + 2, :].rearrange("p a b -> p (a b)"), ps[0:D, 0:2 * D]), m1, nn, prd)
                rS.free[j] = [c2]
                yield
                j, ps, pf = rS.take()
                m2 = mms([(ps[0:D, 0:D], NN[:, 2 * nx, :], NP[:, 0, :])], c2, pt, pf)
                pt = op(dve, lambda q, ps=ps: q.tensor_tensor(NP[:, 0, :], ps[0:D, 0:D], NP[:, 0, :], ALU.add), m2, pt)
                rS.free[j] = [pt]
                prd = [m2]
                nn = [c2]
                cur = nx
                yield
            j, ps, pf = rS.take()
            m = op(pe, lambda q, ps=ps: q.transpose(ps[0:D, 0:D], NP[:, 0, :], IDF[0:D, 0:D]), pt, pf)
            pp = op(dve, lambda q, ps=ps: q.tensor_copy(NP[:, 1, :], ps[0:D, 0:D]), m)
            rS.free[j] = [pp]
            yield
            j, ps, pf = rS.take()
            m = mms([(ps[0:D, 0:C], NP[:, 1, :], VT)], pp, vt, pf)
            zz = op(dve, lambda q, ps=ps: q.tensor_scalar(AT[:, :], ps[0:D, 0:C], di, None, ALU.mult), m, q2, at, c1)
            rS.free[j] = [zz]
            yield
            j, ps, pf = rS.take()
            m = mms([(ps[0:D, 0:C], VT[:, 0:D], AT[:, :])], zz, pf)
            u1 = op(dve, lambda q, ps=ps: q.tensor_tensor(UT[0:D, 0:D], IDF[0:D, 0:D], ps[0:D, 0:D], ALU.subtract), m)
            u2 = op(dve, lambda q, ps=ps: q.tensor_scalar(UT[0:D, D:C], ps[0:D, D:C], -1.0, None, ALU.mult), m)
            rS.free[j] = [u1, u2]
            yield
            t = d_p.go(sp, UT[D:2 * D, :], UT[0:D, :], u1, u2)
            rep = op(dve, lambda q: q.tensor_copy(NP[:, :, :].rearrange("p a b -> p (a b)").rearrange("p (r c) -> p r c", r=4),
                                                  UT[0:D, 256:C].unsqueeze(1).broadcast_to([D, 4, 32])), u2, m, pp)
            j, ps, pf = rS.take()
            for k in range(3):
                src = UT[0:D, k * 128:(k + 1) * 128] if k < 2 else NP[:, :, :].rearrange("p a b -> p (a b)")
                m = op(pe, lambda q, k=k, ps=ps, src=src: q.transpose(ps[:, k * D:(k + 1) * D], src, IDF[0:D, 0:D]), u1, u2, rep, pf)
            p3 = ps[:, 0:3 * D].rearrange("p (k n) -> p k n", k=3)
            h = op(act, lambda q, p3=p3: q.activation(WU[:, 0:3, :], p3, ACT.Copy, scale=WS), m)
            l1 = op(dve, lambda q, p3=p3: q.scalar_tensor_tensor(out=WU[:, 3:5, :], in0=p3[:, 0:2, :], scalar=WS, in1=WU[:, 0:2, :], op0=ALU.mult, op1=ALU.subtract), h)
            l2 = op(dve, lambda q, p3=p3: q.scalar_tensor_tensor(out=WU[64:128, 2, :], in0=p3[64:128, 2, :], scalar=WS, in1=WU[64:128, 2, :], op0=ALU.mult, op1=ALU.subtract), h)
            rS.free[j] = [h, l1, l2]
            tok["U"] = [h, l1, l2, t, u1, u2]
            yield

        onf = ON[:, :, :, :].rearrange("p a b c -> p (a b c)")
        HQ, sq = onf[0:D, 0:C], onf[0:D, C:2 * C]
        NN = OSM[0:D, 0:4 * D].rearrange("p (a b) -> p a b", b=D)
        NP = OSM[0:D, 4 * D:6 * D].rearrange("p (a b) -> p a b", b=D)
        STGV = OSM[0:96, 6 * D:9 * D]
        MGE = sb("MGE", [D, D])
        MLT = sb("MLT", [D, D])
        k1 = op(pool, lambda q: q.memset(MGE[:, :], 1.0))
        k2 = op(pool, lambda q: q.memset(MLT[:, :], 0.0))
        op(pool, lambda q: q.affine_select(out=MGE[:, :], in_=MGE[:, :], compare_op=ALU.is_ge, fill=0.0,
                                           base=0, pattern=[[1, D]], channel_multiplier=-1), k1, k2)
        t_m = op(pool, lambda q: q.affine_select(out=MLT[:, :], in_=MLT[:, :], compare_op=ALU.is_ge, fill=1.0,
                                                 base=0, pattern=[[-1, D]], channel_multiplier=1), k1, k2)

        def rotate(fence):
            cur, et = tok["E"]
            done = []
            for b in range(B):
                sl = slice(64 * (b % 2), 64 * (b % 2) + 64)
                j, ps, pf = rC.take()
                m = mms([(ps[0:D, 0:C], cur[sl, b // 2, 1, :], UT[sl, :])], et, tok["U"], pf, fence)
                v = op(dve, lambda q, ps=ps, b=b: q.tensor_copy(MB[0:D, b, :], ps[0:D, 0:C]), m, fence)
                rC.free[j] = [v]
                done.append(v)
            return done

        def last_layer(fence):
            rZ = Ring([G32[i][0:D, 0:256] for i in range(2)])
            rOut = Ring([Y[i][:, 0:2 * C].rearrange("p (a c) -> p a c", c=C) for i in range(2)])
            o_v = out.rearrange("(t p) c -> p t c", p=128)
            mb = rotate(fence)
            for b in range(B):
                xw = [XW[2 * b], XW[2 * b + 1]]
                yield from to_columns(b % 2, b, X[:, 2 * b:2 * b + 2, :], xw)
                j, ps, pf = rC.take()
                m = mms(products(ps[0:D, 0:256], lambda w: WU[:, w, :], lambda x: XT[:, x, b * 256:(b + 1) * 256], swap=True),
                        TW[2 * b], TW[2 * b + 1], tok["U"], pf)
                iz, z, zf = rZ.take()
                a = op(act, lambda q, z=z, ps=ps: q.activation(z, ps[0:D, 0:256], ACT.Copy, scale=1.0 / WS), m, zf)
                rC.free[j] = [a]
                io, o, of = rOut.take()
                ds = []
                for n in range(2):
                    j, ps, pf = rC.take()
                    m = mms([(ps[:, 0:C], z[:, n * 128:(n + 1) * 128], MB[0:D, b, :])], a, mb, pf)
                    v = op(dve, lambda q, ps=ps, o=o, n=n, b=b: q.tensor_tensor(o[:, n, :], ps[:, 0:C], X[:, 2 * b + n, :], ALU.add), m, xw, of)
                    rC.free[j] = [v]
                    ds.append(v)
                rZ.free[iz] = [m]
                t = d_out[io].go(sp, o_v[:, 2 * b:2 * b + 2, :], o, ds)
                rOut.free[io] = [t]
                yield

        cond_done_v = [None]

        def ada(L):
            w, b = LW[L]["a"]
            yield from cond_rows(I[w], I[b], 6 * C, scr_ada[L], lambda k: 1.0 if k in (1, 4) else 0.0)
            tok["ada", L] = cond_done[-1]

        def vrows():
            yield from cond_rows(I["L3_WT"], I["L3_b"], 7 * C, scr_v, lambda k: 0.0)
            cond_done_v[0] = cond_done[-1]

        rings = [rHB, rA, rC, rO, rS, rA4, rF, *rXB, rY, *rYL, rE, rTM, rG]

        def seq_fence():
            f = last()
            for r in rings:
                r.free = [[f] for _ in r.items]
            for z in (yo_rd, on_rd, dn_rd):
                z[0] = [f]
            return f

        def attention(L, side):
            yield from steps(prep(L, 0), (side, 1.0))
            for b in range(B):
                fin = finish(L, b - 1) if b else iter(())
                nxt = prep(L, b + 1) if b + 1 < B else iter(())
                if L == 1:
                    run(fin)
                    run(regroup(L, b))
                    run(steps(nxt, (side, 0.5)))
                    continue
                yield from steps(attend(L, b), (fin, 1.0), (nxt, 1.6), (side, 0.5))
                run(fin)
                run(nxt)
            yield from steps(finish(L, B - 1), (side, 1.0))
            run(side)

        run(ada(0))
        run(attn_weights(0))
        bg = [chain(mlp_bias(0), w1_load(0, 0), w2_load(0, 0), ada(1), ada(2), vrows()),
              chain(mlp_bias(1), w1_load(1, 0), w2_load(1, 0)),
              chain(mlp_bias(2), w1_load(2, 0), w2_load(2, 0))]
        for L in range(3):
            run(attention(L, bg[L]))
            if L == 0:
                gates()
            f = seq_fence()
            side = chain(attn_weights(L + 1)) if L < 2 else iter(())
            if L == 0:
                side = chain(side, expm_steps(), householder())
            run(steps(mlp(L, f), (side, 0.9)))
            run(side)
            ad_rd[0] = ad_rd[1] = ae_rd[0] = ae_rd[1] = [last()]
            f = seq_fence()
            if stop == L:
                break
        if stop is None:
            run(last_layer(f))
        else:
            o_v = out.rearrange("(t p) c -> p t c", p=128)
            d_out[0].go(sp, o_v, X[:, :, :], f)
        for d in d_out:
            if d.count:
                put(sp, None, [(d.sem, d.count)], None)
        for d in (*d_os, *d_ho):
            put(sp, None, [(d.sem, d.count)], None)

        block = ctx.enter_context(nc.Block())

        def issue(e, q):
            for waits, fn, inc in e.queue:
                for s, v in waits:
                    q.wait_ge(s, v)
                if fn is not None:
                    ins = fn(q)
                    if inc is not None:
                        ins.then_inc(*inc)

        @block.tensor
        def _(q):
            issue(pe, q)

        @block.vector
        def _(q):
            issue(dve, q)

        @block.scalar
        def _(q):
            issue(act, q)

        @block.gpsimd
        def _(q):
            issue(pool, q)

        @block.sync
        def _(q):
            issue(sp, q)


def layouts(inp):
    def r(a, *s):
        return np.ascontiguousarray(a).reshape(*s)

    I = {"x": r(inp["x"], B * T, C), "cT": np.ascontiguousarray(np.asarray(inp["cond_1152"]).T)}
    for k, v in inp.items():
        v = np.asarray(v)
        if k in ("x", "cond_1152"):
            continue
        L, n = k[:2], k[8:]
        if k == "L3_cond_P":
            I["PT"] = np.ascontiguousarray(v.T)
        elif k == "L3_cond_W":
            I["L3_WT"] = np.ascontiguousarray(v.T)
        elif k == "L0_cond_b1":
            I["L0_b1T"] = np.ascontiguousarray(v.reshape(NE, 9, 128).transpose(2, 0, 1))
        elif k in ("L1_cond_fc1_b", "L2_cond_b_fc1"):
            I[f"{L}_b1T"] = np.ascontiguousarray(v.reshape(9, 128).T)
        else:
            I[f"{L}_{n}"] = np.ascontiguousarray(v)
    return I


def make(nc, arrays, stop=None):
    args = {k: nc.dram_tensor(f"in_{k}", a.shape, mybir.dt.from_np(a.dtype), kind="ExternalInput").ap() for k, a in arrays.items()}
    out = nc.dram_tensor("out_0", (B * T, C), F32, kind="ExternalOutput").ap()
    scr_ada = nc.dram_tensor("scr_ada", (3, B, 6 * C), F32, kind="Internal").ap()
    scr_v = nc.dram_tensor("scr_v", (B, 7 * C), F32, kind="Internal").ap()
    scr_o = nc.dram_tensor("scr_o", (B, NH, T, HD), F32, kind="Internal").ap()
    program(nc, args, out, scr_ada, scr_v, scr_o, stop)


def kernel(**inputs):
    import concourse.bacc as _bacc
    from concourse.bass_utils import run_bass_kernel_spmd as _run

    nc = _bacc.Bacc("TRN2", target_bir_lowering=False, num_devices=1)
    arrays = layouts(inputs)
    make(nc, arrays)
    r = _run(nc, [{f"in_{k}": a for k, a in arrays.items()}], core_ids=[0])
    return r.results[0]["out_0"].reshape(B, T, C)
```

```python
from contextlib import ExitStack

import numpy as np
import concourse.bass as bass
from concourse import mybir

F32 = mybir.dt.float32
F16 = mybir.dt.float16
ALU = mybir.AluOpType
ACT = mybir.ActivationFunctionType
AX = mybir.AxisListType

B, T, C, NH, HD, HID, NE = 8, 256, 288, 16, 18, 1152, 4
NT = B * T // 128
WS = 64.0
QS = float(HD) ** -0.5
EPS = 1e-6
D = 64
NSQ = 12
TINY = 0.22
TAB = 1.3
DMAT = 3.0
LAT = 0.1
SLACK = -0.5
BIAS = 0.2
PB = 0.0
DB = 1.0
RA, RB = 0, 3
RP, RF = (1, 0, 1), (2, 0, 2)
RANKS = 9
R1F, R1N, R1M = 2, 1, 1.5
NP1 = 16
ZS = (256, 384, 512, 640, 768, 896)
AR = 17664
PRODUCTS = [(0, 0), (1, 1), (2, 2), (3, 0), (4, 1), (0, 3), (1, 4)]


class Engine:

    def __init__(self, name, sem):
        self.name, self.sem, self.count, self.seen, self.queue = name, sem, 0, {}, []
        self.clock = 0.0


def flat(deps):
    for d in deps:
        if d is None:
            continue
        if isinstance(d, list) or not (len(d) == 2 and isinstance(d[1], int)):
            yield from flat(d)
        else:
            yield d


class Ring:

    late = None

    def __init__(self, items):
        self.items, self.free = items, [[] for _ in items]

    def take(self):
        i = min((i for i, f in enumerate(self.free) if f is not None), key=lambda i: self.late(self.free[i]))
        tokens, self.free[i] = self.free[i], None
        return i, self.items[i], tokens

    def held(self):
        return all(f is None for f in self.free)


def chain(*parts):
    for p in parts:
        yield from p


def slot(ring):
    while ring.held():
        yield "wait"


def part(g, n):
    for _ in range(n):
        v = next(g, "end")
        if v == "end":
            return
        yield v


def run(g):
    for _ in g:
        pass


def program(nc, I, out, scr_ada, scr_v, scr_o, scr_w1, scr_w2, stop=None):
    ctx = ExitStack()
    with ctx:
        def sb(name, shape, dt=F32):
            return ctx.enter_context(nc.sbuf_tensor(name, shape, dt))

        def sem(name):
            return ctx.enter_context(nc.semaphore(name))

        eng = {n: Engine(n, sem(f"s_{n}")) for n in ("tensor", "vector", "scalar", "gpsimd", "sync")}
        pe, dve, act, pool, sp = (eng[n] for n in ("tensor", "vector", "scalar", "gpsimd", "sync"))

        price = {"tensor": 0.1, "vector": 0.45, "scalar": 0.6, "gpsimd": 0.7, "sync": 0.05}
        ends, newest = {}, [0.0]

        def put(e, fn, deps, inc, c=None, token=None):
            waits = []
            for s, v in flat(deps):
                e.clock = max(e.clock, ends.get((id(s), v), 0.0) + LAT)
                if e.seen.get(id(s), 0) < v:
                    e.seen[id(s)] = v
                    waits.append((s, v))
            best = {}
            for s, v in waits:
                best[id(s)] = (s, v)
            e.clock += price[e.name] if c is None else c
            if token is not None:
                ends[id(token[0]), token[1]] = e.clock + (DMAT if inc[1] == 16 else 0.0)
                newest[0] = max(newest[0], ends[id(token[0]), token[1]])
            e.queue.append((list(best.values()), fn, inc))

        def op(e, fn, *deps, c=None):
            e.count += 1
            put(e, fn, deps, (e.sem, 1), c, (e.sem, e.count))
            return (e.sem, e.count)

        def sooner(deps, *choices):
            at = eta(deps)
            return min(choices, key=lambda x: max(x[0].clock, at) + x[1])

        def copy(dst, src, c_act, c_dve, *deps):
            e, c = sooner(deps, (act, c_act), (dve, c_dve))
            if e is act:
                return op(act, lambda q: q.activation(dst, src, ACT.Copy), deps, c=c)
            return op(dve, lambda q: q.tensor_copy(dst, src), deps, c=c)

        table = [None]

        def tables(kind):
            if table[0] != kind:
                table[0] = kind
                act.clock += TAB

        def tiny(e, fn, *deps):
            return op(e, fn, *deps, c=TINY)

        def quiet(e, fn, *deps, c=None):
            put(e, fn, deps, None, c)

        class Dma:

            def __init__(self, name):
                self.sem, self.count = sem(name), 0

            def go(self, e, dst, src, *deps, **how):
                self.count += 16
                put(e, lambda q, dst=dst, src=src: q.dma_start(dst, src, **how), deps, (self.sem, 16),
                    None, (self.sem, self.count))
                return (self.sem, self.count)

        def mms(items, *deps):
            n = len(items)
            for k, (o, l, r) in enumerate(items):
                fn = lambda q, o=o, l=l, r=r, a=(k == 0), z=(k == n - 1): q.matmul(o, l, r, start=a, stop=z)
                c = max(0.05, int(np.prod(r.shape[1:])) / 2400 * (4 if r.dtype == F32 else 1) + 0.03)
                if k == n - 1:
                    return op(pe, fn, deps if k == 0 else [], c=c)
                quiet(pe, fn, deps if k == 0 else [], c=c)

        def last():
            return [(e.sem, e.count) for e in (pe, dve, act, pool) if e.count]

        def eta(tokens):
            return max((ends.get((id(s), v), 0.0) for s, v in flat(tokens)), default=0.0)

        Ring.late = staticmethod(eta)

        X = sb("X", [128, NT, C])
        XT = sb("XT", [128, 5, NT * 128], F16)
        W1 = sb("W1", [128, 5, HID], F16)
        W2 = sb("W2", [128, 19, C], F16)
        WQ = sb("WQ", [128, 5, 3 * C], F16)
        WP = sb("WP", [128, 5, C], F16)
        WG = sb("WG", [128, 5, NE], F16)
        STG = [sb(f"STG{i}", [128, 1152]) for i in range(2)]
        ADB = sb("ADB", [128, 10 * C])
        AD1 = [ADB[:, 2 * i * C:(2 * i + 2) * C] for i in range(2)]
        AD2 = [ADB[:, (4 + 3 * i) * C:(7 + 3 * i) * C] for i in range(2)]
        G2 = sb("G2", [128, 2, C])
        H = sb("H", [128, 9, 2, 512], F16)
        ARENA = sb("ARENA", [128, AR], F16)
        QT = [sb(f"QT{i}", [128, 8, 256], F16) for i in range(2)]
        KZ = [sb(f"KZ{i}", [128, 8, 2, 256], F16) for i in range(2)]
        VB = [sb(f"VB{i}", [128, 2, NH, 37], F16) for i in range(2)]
        QB = sb("QB", [128, NH, 64], F16)
        KB = sb("KB", [128, NH, 64], F16)
        G32 = [sb(f"G32_{i}", [128, 512]) for i in range(2)]
        TM = [sb(f"TM{i}", [128, C]) for i in range(2)]
        ONES = sb("ONES", [128, 128], F16)
        CT = sb("CT", [96, 3, B])
        CS = sb("CS", [96, 3, B])
        OSM = sb("OSM", [96, 2 * C])
        OS = [OSM[0:B, i * C:(i + 1) * C] for i in range(2)]
        IDF = sb("IDF", [128, 128])
        IDH = sb("IDH", [128, 128], F16)
        ID2 = sb("ID2", [128, D])
        STS = [sb(f"ST{w}", [128, 2, 6]) for w in range(2)]
        MVS = [sb(f"MV{w}", [128, 2, 2]) for w in range(2)]
        RSS = [sb(f"RS{w}", [128, 2, 2]) for w in range(2)]
        PH = sb("PH", [128, 2])
        NM = sb("NM", [128, 2, 2, 8], F16)
        MT = sb("MT", [16, 256], F16)
        DN = sb("DN", [128, 4, 8])
        LG = sb("LG", [128, NT, NE])
        CWA = sb("CW", [128, NT, NE])
        CWSA = sb("CWS", [128, NT, NE])
        LT = sb("LT", [128, 4, 16])
        LM = sb("LM", [128, 4, 16])
        TRI = sb("TRI", [128, 16])
        L1 = sb("L1", [128, 4])
        EX = sb("EX", [128, 4, 2, D])
        EY = sb("EY", [128, 4, 2, D])
        EW = sb("EW", [128, 4, 2, D])
        AT = sb("AT", [D, C])
        TI = sb("TI", [D, D])
        NMK = sb("NMK", [D, D])
        HS = sb("HS", [D, 8])
        N2 = sb("N2", [D, 2])
        UT = sb("UT", [128, C])
        WU = sb("WU", [128, 5, D], F16)

        arena = ARENA[:, :]
        used = [0]

        def over(shape, dt=F32):
            n = int(np.prod(shape)) * (2 if dt == F32 else 1)
            a = arena[:, used[0]:used[0] + n]
            used[0] += n
            if dt == F32:
                a = a.bitcast(F32)
            if len(shape) == 2:
                a = a.rearrange("p (a b) -> p a b", b=shape[1])
            elif len(shape) == 3:
                a = a.rearrange("p (a b c) -> p a b c", b=shape[1], c=shape[2])
            elif len(shape) == 4:
                a = a.rearrange("p (a b c d) -> p a b c d", b=shape[1], c=shape[2], d=shape[3])
            return a

        E32 = [over([1024]) for _ in range(2)]
        PHI = [over([2, 2, 256], F16) for _ in range(2)]
        PLO = [over([2, 2, 256], F16) for _ in range(2)]
        Y = [over([3 * C]) for _ in range(2)]
        XB = [over([2, 640], F16) for _ in range(2)]
        YL = [over([2, C]) for _ in range(2)]
        YO = over([2, C])
        ON = sb("ON", [128, 4, 2, 4 * HD])
        assert used[0] == AR, used[0]
        small = arena[:, 0:8192].bitcast(F32)
        rHB = Ring([small[:, i * 1152:(i + 1) * 1152] for i in range(3)])
        SC = small[:, 3456:3712].rearrange("p (h k) -> p h k", k=NH)
        SM = small[:, 3712:3744]

        P = [ctx.enter_context(nc.psum_tensor(f"P{i}", [128, 512], F32)) for i in range(8)]
        rA, rC, rO = Ring([p[:, :] for p in P[0:2]]), Ring([p[:, :] for p in P[2:7]]), Ring([P[7][:, :]])
        rU = rC
        rXB, rY, rYL = [Ring([x]) for x in XB], Ring([*Y, QT[1][:, :, :].rearrange("p a b -> p (a b)").bitcast(F32)[:, 0:3 * C]]), [Ring([y]) for y in YL]
        rE, rTM, rG, rOS = Ring([0, 1]), Ring([t[:, :] for t in TM]), Ring([g[:, :] for g in G32]), Ring(OS)
        STG += [H[:, :, :, :].rearrange("p a b c -> p (a b c)")[:, 2304 * i:2304 * i + 2304].bitcast(F32) for i in range(4)]
        rSTG = Ring(range(6))
        d_stg = [Dma(f"d_stg{i}") for i in range(6)]
        d_os = [Dma(f"d_os{i}") for i in range(2)]
        d_ad = [Dma(f"d_ad{i}") for i in range(2)]
        d_ae = [Dma(f"d_ae{i}") for i in range(2)]
        d_mt = [Dma(f"d_mt{i}") for i in range(2)]
        d_ho = [Dma(f"d_ho{i}") for i in range(2)]
        d_yo = Dma("d_yo")
        d_w = [Dma(f"d_w{i}") for i in range(2)]
        d_s = [Dma(f"d_s{i}") for i in range(2)]
        d_out = [Dma(f"d_out{i}") for i in range(2)]
        d_in, d_v, d_p, d_g2, d_c = Dma("d_in"), Dma("d_v"), Dma("d_p"), Dma("d_g2"), Dma("d_c")

        XW = [[] for _ in range(NT)]
        XR = [[] for _ in range(NT)]
        TW = [[] for _ in range(NT)]
        TR = [[] for _ in range(NT)]

        k = [op(pool, lambda q: q.memset(IDF[:, :], 0.0)), op(pool, lambda q: q.memset(NMK[:, :], 0.0)),
             op(pool, lambda q: q.memset(TRI[:, :], 0.0)), op(pool, lambda q: q.memset(ID2[:, :], 0.0)),
             op(pool, lambda q: q.memset(PH[:, :], -0.5))]
        t_idf = op(pool, lambda q: q.affine_select(out=IDF[:, :], in_=IDF[:, :], compare_op=ALU.not_equal, fill=1.0,
                                                   base=0, pattern=[[-1, 128]], channel_multiplier=1), k)
        t_nmk = op(pool, lambda q: q.affine_select(out=NMK[:, :], in_=NMK[:, :], compare_op=ALU.is_ge, fill=-1.0,
                                                   base=0, pattern=[[1, D]], channel_multiplier=-1), k)
        t_tri = op(pool, lambda q: q.affine_select(
            out=TRI[:, :].rearrange("p (e j) -> p e j", e=4), in_=TRI[:, :].rearrange("p (e j) -> p e j", e=4),
            compare_op=ALU.is_ge, fill=1.0, base=0, pattern=[[-1, 4], [1, 4]], channel_multiplier=0), k)
        t_id2 = op(pool, lambda q: q.affine_select(out=ID2[:, :], in_=ID2[:, :], compare_op=ALU.not_equal, fill=1.0,
                                                   base=0, pattern=[[-1, D]], channel_multiplier=1), k)
        t_id2 = op(pool, lambda q: q.affine_select(out=ID2[:, :], in_=ID2[:, :], compare_op=ALU.not_equal, fill=1.0,
                                                   base=-D, pattern=[[-1, D]], channel_multiplier=1), t_id2)
        t_idh = op(dve, lambda q: q.tensor_copy(IDH[:, :], IDF[:, :]), t_idf)
        t_qb = [op(dve, lambda q: q.memset(QB[:, :, :], 0.0))]
        t_kb = op(dve, lambda q: q.memset(KB[:, :, :], 0.0))
        t_kb = [op(dve, lambda q: q.memset(KB[:, :, 54:55], 1.0), t_kb)]
        t_kz = [op(pool, lambda q, i=i: q.memset(KZ[i][:, :, :, :], 0.0)) for i in range(2)]
        t_on = op(dve, lambda q: q.memset(ONES[:, :], 0.0))
        t_on = [op(dve, lambda q: q.memset(ONES[0:1, :], 1.0), t_on), op(dve, lambda q: q.memset(ONES[32:33, :], 1.0), t_on)]
        t_xb = [op(dve, lambda q, i=i: q.memset(XB[i][:, :, 352:384], 0.0)) for i in range(2)]
        t_xb = [op(dve, lambda q, i=i: q.memset(XB[i][:, :, 352:354], 1.0), t_xb) for i in range(2)]
        t_vb = [op(dve, lambda q, i=i: q.memset(VB[i][:, :, :, 18:19], 1.0)) for i in range(2)]

        x_v = I["x"].rearrange("(t p) c -> p t c", p=128)
        t_c = d_c.go(sp, CT[:, :, :], I["cT"].rearrange("(k p) b -> p k b", p=96))
        t_at = d_p.go(sp, AT[:, :], I["PT"])
        for q4 in range(4):
            t_x = d_in.go(act, X[:, 4 * q4:4 * q4 + 4, :], x_v[:, 4 * q4:4 * q4 + 4, :])
        for t in range(NT):
            XW[t] = [t_x]
        t_cs = op(act, lambda q: q.activation(CS[:, :, :], CT[:, :, :], ACT.Silu), t_c)

        def cond_rows(w, bias, n, dst, first, name=None):
            w_v = w.rearrange("(k p) n -> p k n", p=96)
            toks = []
            for k in range(n // C):
                i, _, free = rSTG.take()
                W = STG[i][0:96, 0:3 * C].rearrange("p (k n) -> p k n", k=3)
                Bb = STG[i][0:B, 3 * C:4 * C]
                d_stg[i].go(sp, W, w_v[:, :, k * C:(k + 1) * C], free)
                t = d_stg[i].go(sp, Bb, bias[k * C:(k + 1) * C].partition_broadcast(B))
                yield
                yield from slot(rC)
                j, ps, pf = rC.take()
                m = mms([(ps[0:B, 0:C], CS[:, q, :], W[:, q, :]) for q in range(3)], t, t_cs, pf)
                o, _, of = rOS.take()
                a = op(dve, lambda q, o=o, ps=ps, Bb=Bb, f=first(k): q.scalar_tensor_tensor(
                    out=OS[o][:, :], in0=ps[0:B, 0:C], scalar=f, in1=Bb, op0=ALU.add, op1=ALU.add), m, t, of)
                rC.free[j], rSTG.free[i] = [a], [m, a]
                s = d_os[o].go(sp, dst[:, k * C:(k + 1) * C], OS[o][:, :], a)
                rOS.free[o] = [s]
                toks = [x for x in toks if x[0] is not s[0]] + [s]
                tok[name, k] = toks
                yield
            cond_done.append(toks)

        cond_done = []

        def split_cols(dst, before, w, cols, scales, bias):
            done = []
            for blk in range(3):
                i, S, free = rSTG.take()
                S = STG[i]
                if blk < 2:
                    t = d_stg[i].go(sp, S[:, 0:cols], w[blk * 128:(blk + 1) * 128, :], free)
                else:
                    for g in range(3):
                        t = d_stg[i].go(sp, S[32 * g:32 * g + 32, 0:cols], w[256:288, :], free if g == 0 else [])
                    if bias is not None:
                        t = d_stg[i].go(sp, S[96:128, 0:cols], bias.partition_broadcast(32))
                yield
                fin = []
                for a, b, s in scales:
                    if blk < 2:
                        h, l = dst[:, blk, a:b], dst[:, 3 + blk, a:b]
                        x = op(act, lambda q, h=h, v=S[:, a:b], s=s: q.activation(h, v, ACT.Copy, scale=s), t, before)
                        y = op(dve, lambda q, h=h, l=l, v=S[:, a:b], s=s: q.scalar_tensor_tensor(
                            out=l, in0=v, scalar=s, in1=h, op0=ALU.mult, op1=ALU.subtract), x, t, before)
                        fin += [x, y]
                    else:
                        z = 96 if bias is None else 128
                        x = op(act, lambda q, h=dst[0:z, 2, a:b], v=S[0:z, a:b], s=s: q.activation(h, v, ACT.Copy, scale=s), t, before)
                        y = op(dve, lambda q, l=dst[64:96, 2, a:b], v=S[64:96, a:b], s=s: q.scalar_tensor_tensor(
                            out=l, in0=v, scalar=s, in1=l, op0=ALU.mult, op1=ALU.subtract), x, t, before)
                        fin += [x, y]
                        if bias is not None:
                            y = op(dve, lambda q, l=dst[96:128, 2, a:b], v=S[96:128, a:b], s=s: q.scalar_tensor_tensor(
                                out=l, in0=v, scalar=s, in1=l, op0=ALU.mult, op1=ALU.subtract), x, t, before)
                            x = op(act, lambda q, h=dst[96:97, 2, a:b], v=S[96:97, a:b], s=s: q.activation(h, v, ACT.Copy, scale=s), y, t)
                            fin += [x, y]
                if blk == 2 and bias is None:
                    fin.append(op(dve, lambda q: q.memset(dst[96:128, 2, 0:cols], 0.0), before))
                rSTG.free[i] = fin
                done += fin
                yield
            tok["split"] = done

        LW = [dict(q=("L0_w_qkv", "L0_b_qkv"), p=("L0_w_proj", "L0_b_proj"), a=("L0_w_adaln", "L0_b_adaln"), ne=4,
                   act=ACT.Gelu_apprx_tanh),
              dict(q=("L1_qkv_w", "L1_qkv_b"), p=("L1_proj_w", "L1_proj_b"), a=("L1_ada_w", "L1_ada_b"), ne=1,
                   act=ACT.Gelu),
              dict(q=("L2_W_qkv", "L2_b_qkv"), p=("L2_W_proj", "L2_b_proj"), a=("L2_W_ada", "L2_b_ada"), ne=1,
                   act=ACT.Gelu_apprx_tanh)]

        def mlp_w(L, e):
            if L == 0:
                return I["L0_w1"][e], I["L0_w2"][e], I["L0_b1"][e], I["L0_b2"][e]
            n = ("L1_fc1_w", "L1_fc2_w", "L1_fc1_b", "L1_fc2_b") if L == 1 else ("L2_W_fc1", "L2_W_fc2", "L2_b_fc1", "L2_b_fc2")
            return I[n[0]], I[n[1]], I[n[2]], I[n[3]]

        tok = {}
        wq_rd, wp_rd, w1_rd, w2_rd = [[]], [[]], [[]], [[]]

        def wq_load(L):
            w, b = LW[L]["q"]
            yield from split_cols(WQ, wq_rd[0], I[w], 3 * C, [(0, C, WS * QS), (C, 3 * C, WS)], I[b])
            tok["wq", L] = tok["split"]

        def wp_load(L):
            w, b = LW[L]["p"]
            yield from split_cols(WP, wp_rd[0], I[w], C, [(0, C, WS)], I[b])
            tok["wp", L] = tok["split"]

        def wg_load():
            yield from split_cols(WG, [], I["L0_w_gate"], NE, [(0, NE, WS)], None)
            tok["wg"] = tok["split"]

        saved = {}

        def w1_load(L, e):
            if (1, e) in saved and L == 0:
                tok["w1"] = [d_w[0].go(sp, W1[:, :, :], scr_w1[e], w1_rd[0], saved[1, e])]
                w1_rd[0] = []
                yield
                return
            yield from split_cols(W1, w1_rd[0], mlp_w(L, e)[0], HID, [(0, HID, WS)], mlp_w(L, e)[2])
            tok["w1"] = tok["split"]
            if L == 0:
                saved[1, e] = d_s[0].go(sp, scr_w1[e], W1[:, :, :], tok["w1"])
                w1_rd[0] = [saved[1, e]]

        def w2_load(L, e):
            if (2, e) in saved and L == 0:
                tok["w2"] = [d_w[1].go(sp, W2[:, :, :], scr_w2[e], w2_rd[0], saved[2, e])]
                w2_rd[0] = []
                yield
                return
            w = mlp_w(L, e)[1].rearrange("(m p) n -> p m n", p=128)
            before = w2_rd[0]
            done = []
            for c in range(3):
                i, _, free = rSTG.take()
                S = STG[i][:, 0:3 * C].rearrange("p (m n) -> p m n", m=3)
                t = d_stg[i].go(sp, S, w[:, 3 * c:3 * c + 3, :], free)
                if c == 0:
                    t = d_stg[i].go(sp, STG[i][:, 3 * C:4 * C], mlp_w(L, e)[3].partition_broadcast(128))
                yield
                h, l = (W2[:, 6 * c + s:6 * c + s + 5:2, :] for s in range(2))
                x = op(act, lambda q, h=h, S=S: q.activation(h, S, ACT.Copy, scale=WS), t, before)
                y = op(dve, lambda q, h=h, l=l, S=S: q.scalar_tensor_tensor(
                    out=l, in0=S, scalar=WS, in1=h, op0=ALU.mult, op1=ALU.subtract), x, t, before)
                fin = [x, y]
                if c == 0:
                    Sb = STG[i][:, 3 * C:4 * C]
                    x = op(act, lambda q, Sb=Sb: q.activation(W2[:, 18, :], Sb, ACT.Copy, scale=WS), t, before)
                    y = op(dve, lambda q, Sb=Sb: q.scalar_tensor_tensor(
                        out=W2[32:64, 18, :], in0=Sb[32:64, :], scalar=WS, in1=W2[32:64, 18, :], op0=ALU.mult, op1=ALU.subtract), x, t)
                    fin += [x, y]
                rSTG.free[i] = fin
                done += fin
                yield
            tok["w2"] = done
            if L == 0:
                saved[2, e] = d_s[1].go(sp, scr_w2[e], W2[:, :, :], done)
                w2_rd[0] = [saved[2, e]]

        def to_columns(w, b, y, ytok):
            i, xb, free = rXB[w].take()
            a1 = op(act, lambda q: q.activation(xb[:, :, 0:C], y, ACT.Copy), ytok, free, c=0.7)
            a2 = op(act, lambda q: q.activation(xb[:, :, 320:352], y[:, :, 256:C], ACT.Copy), ytok, c=0.25)
            yield [a1]
            d1 = op(dve, lambda q: q.tensor_tensor(xb[:, :, 384:640], y[:, :, 0:256], xb[:, :, 0:256], ALU.subtract), a1, ytok, free, c=0.6)
            p1 = op(pool, lambda q: q.tensor_tensor(xb[:, :, 288:320], y[:, :, 256:C], xb[:, :, 256:288], ALU.subtract), a1, ytok, free, c=0.25)
            yield
            toks = []
            for n in range(2):
                t = 2 * b + n
                yield from slot(rC)
                j, ps, pf = rC.take()
                psh = ps.bitcast(F16)
                for k in range(5):
                    fn = lambda q, psh=psh, k=k, n=n: q.transpose(psh[:, k * 128:(k + 1) * 128], xb[:, n, k * 128:(k + 1) * 128], IDH[:, :])
                    if k < 4:
                        quiet(pe, fn, [a1, a2, d1, p1, pf, t_idh, t_xb] if k == 0 else [])
                    else:
                        m = op(pe, fn)
                yield [m]
                dst = XT[:, :, t * 128:(t + 1) * 128]
                src = psh[:, 0:640].rearrange("p (k t) -> p k t", k=5)
                v = copy(dst, src, 0.75 + BIAS, 0.75, m, TR[t])
                rC.free[j] = [v]
                TW[t], TR[t] = [v], []
                toks.append(m)
                yield "free" if n == 0 else None
            rXB[w].free[i] = toks
            tok["read"] = [a1, a2, d1, p1]

        def products(ps, lhs, rhs, swap=False):
            return [(ps, lhs(x), rhs(w)) if not swap else (ps, lhs(w), rhs(x)) for x, w in PRODUCTS]

        def layernorm(w, b, sc, sh, adt):
            i, yl, free = rYL[w].take()
            ST, MV, RS = STS[w], MVS[w], RSS[w]
            ts = []
            for n in range(2):
                t = 2 * b + n
                s = op(dve, lambda q, n=n, t=t: q.bn_stats(ST[:, n, :], X[:, t, :]), XW[t], tok.get(("st", w)), c=0.38)
                s = op(dve, lambda q, n=n: q.bn_aggr(MV[:, n, :], ST[:, n, :]), s, tok.get(("mv", w)), c=0.08)
                ts.append(s)
            tok["st", w] = ts
            p = op(pool, lambda q: q.tensor_scalar(RS[:, 0, :], MV[:, :, 1], EPS, None, ALU.add), ts, tok.get(("mv", w)), c=0.1)
            p = op(pool, lambda q: q.tensor_tensor(RS[:, 1, :], RS[:, 0, :], PH[:, :], ALU.pow), p, c=0.1)
            yield
            r = []
            for n in range(2):
                t = 2 * b + n
                y = yl[:, n, :]
                a = op(dve, lambda q, n=n, t=t, y=y: q.scalar_tensor_tensor(
                    out=y, in0=X[:, t, :], scalar=MV[:, n, 0:1], in1=sc, op0=ALU.subtract, op1=ALU.mult), ts, adt, XW[t], free)
                XR[t] = XR[t] + [a]
                r.append(a)
            for n in range(2):
                y = yl[:, n, :]
                r[n] = op(dve, lambda q, n=n, y=y: q.scalar_tensor_tensor(
                    out=y, in0=y, scalar=RS[:, 1, n:n + 1], in1=sh, op0=ALU.mult, op1=ALU.add), r[n], p)
            tok["mv", w] = r
            yield
            yield from to_columns(w, b, yl, r)
            rYL[w].free[i] = tok["read"]
            tok["lnd"] = r

        qt_rd, kz_rd, vb_rd = [[], []], [[], []], [[], []]
        qb_rd, kb_rd, nm_rd, mt_rd = [[]], [[]], [[]], [[]]
        ad_rd, ae_rd = [[], []], [[], []]

        flags = set()

        def prep(L, b):
            if L:
                yield from ms.wait(L - 1, b)
            u = b % 2
            adt = d_ad[u].go(sp, AD1[u], scr_ada[L, b, 0:2 * C].partition_broadcast(128), ad_rd[u], tok[("ada", L), 1])
            yield
            yield from layernorm(0, b, AD1[u][:, C:2 * C], AD1[u][:, 0:C], adt)
            ad_rd[u] = [tok["lnd"]]
            wr_q, wr_k, wr_v = [], [], []
            for n in range(2):
                t = 2 * b + n

                def columns(s):
                    j, ps, pf = rC.take()
                    m = mms(products(ps[:, 0:C], lambda x: XT[:, x, t * 128:(t + 1) * 128],
                                     lambda w: WQ[:, w, s * C:(s + 1) * C]), TW[t], tok["wq", L], pf)
                    return j, ps[:, 0:C], m

                if L == 1:
                    yield from slot(rY)
                    iy, y, yf = rY.take()
                    ev = []
                    for s in range(3):
                        yield from slot(rC)
                        j, ps, m = columns(s)
                        yield [m]
                        dst = y[:, s * C:(s + 1) * C]
                        ev.append(op(act, lambda q, ps=ps, dst=dst: q.activation(dst, ps, ACT.Copy, scale=1.0 / WS), m, yf))
                        rC.free[j] = [ev[-1]]
                        yield
                    TR[t] = [m]
                    wq_rd[0] = [m]
                    tok["y", b, n] = (iy, y, ev)
                    if n == 1:
                        flags.add(("q", b))
                    continue
                qh = QB[:, :, 0:54].rearrange("p h (r d) -> p h r d", d=HD)[:, :, 0:3:2, :]
                kh = KB[:, :, 0:36].rearrange("p h (r d) -> p h r d", d=HD)
                vh, vl = VB[u][:, n, :, 0:18], VB[u][:, n, :, 19:37]
                got = []
                for s, hi, one, lo, dep in ((0, qh, QB[:, :, 0:18], QB[:, :, 18:36], [qb_rd[0], t_qb]),
                                            (1, kh, KB[:, :, 0:18], KB[:, :, 36:54], [kb_rd[0], t_kb]),
                                            (2, vh, vh, vl, [vb_rd[u], t_vb])):
                    yield from slot(rC)
                    j, ps, m = columns(s)
                    yield [m]
                    p3 = ps.rearrange("p (h d) -> p h d", d=HD)
                    two = p3.unsqueeze(2).broadcast_to([128, NH, 2, HD]) if s < 2 else p3
                    a = op(act, lambda q, hi=hi, two=two: q.activation(hi, two, ACT.Copy, scale=1.0 / WS), m, dep, c=0.6)
                    yield [a]
                    d = op(dve, lambda q, lo=lo, p3=p3, one=one: q.scalar_tensor_tensor(
                        out=lo, in0=p3, scalar=1.0 / WS, in1=one, op0=ALU.mult, op1=ALU.subtract), a, dep, c=0.4)
                    rC.free[j] = [a, d]
                    got.append([a, d])
                    yield "free"
                TR[t] = [m]
                wq_rd[0] = [m]
                wr_v += got[2]
                yield
                for src, deps, rd in ((QB, [got[0], t_qb], qb_rd), (KB, [got[1], t_kb], kb_rd)):
                    yield from slot(rC)
                    j, ps, pf = rC.take()
                    psh = ps.bitcast(F16)
                    for c in range(8):
                        fn = lambda q, psh=psh, c=c, src=src: q.transpose(
                            psh[:, c * 128:(c + 1) * 128], src[:, 2 * c:2 * c + 2, :].rearrange("p a b -> p (a b)"), IDH[:, :])
                        if c < 7:
                            quiet(pe, fn, [deps, pf, t_idh] if c == 0 else [])
                        else:
                            m = op(pe, fn)
                    rd[0] = [m]
                    yield [m]
                    s3 = psh.rearrange("p (c t) -> p c t", c=8)
                    if src is QB:
                        v = copy(QT[u][:, :, n * 128:(n + 1) * 128], s3, 1.05 + BIAS, 1.15, m, qt_rd[u])
                        wr_q.append(v)
                        rC.free[j] = [v]
                    else:
                        v1 = copy(KZ[u][0:64, :, 0, n * 128:(n + 1) * 128], s3[0:64], 1.05 + BIAS, 1.15, m, kz_rd[u], t_kz)
                        v2 = copy(KZ[u][64:128, :, 1, n * 128:(n + 1) * 128], s3[64:128], 1.05 + BIAS, 1.15, m, kz_rd[u], t_kz, v1)
                        wr_k += [v1, v2]
                        rC.free[j] = [v1, v2]
                    yield "free" if src is QB else None
            if L == 1:
                return
            tok["v", b] = wr_v
            mx = []
            for c in range(8):
                for n in range(2):
                    yield from slot(rC)
                    j, ps, pf = rC.take()
                    m = mms([(ps, QT[u][:, c, n * 128:(n + 1) * 128], KZ[u][:, c, :, :].rearrange("p a b -> p (a b)"))],
                            wr_q, wr_k, pf, t_kz)
                    yield [m]
                    v = op(dve, lambda q, ps=ps, n=n, c=c: q.tensor_reduce(
                        NM[:, n, :, c], ps.rearrange("p (a k) -> p a k", a=2), AX.X, ALU.max, negate=True), m, nm_rd[0], c=0.62)
                    rC.free[j] = [v]
                    mx.append(v)
            yield [v]
            yield from slot(rC)
            j, ps, pf = rC.take()
            psh = ps.bitcast(F16)
            for n in range(2):
                m = op(pe, lambda q, psh=psh, n=n: q.transpose(
                    psh[0:16, n * 128:(n + 1) * 128], NM[:, n, :, :].rearrange("p a b -> p (a b)"), IDH[:, :]), mx, pf, t_idh)
            nm_rd[0] = [m]
            yield [m]
            v = op(act, lambda q, psh=psh: q.activation(MT[:, :], psh[0:16, 0:256], ACT.Copy), m, mt_rd[0], c=0.4)
            rC.free[j] = [v]
            d_mt[u].go(sp, QT[u][54:55, :, :], MT[0:8, :], v, m)
            t2 = d_mt[u].go(sp, QT[u][118:119, :, :], MT[8:16, :])
            mt_rd[0] = [t2]
            tok["qk", b] = [wr_q, wr_k, t2]
            yield

        on_rd, dn_rd, yo_rd = [[]], [[]], [[]]
        hs_free = {"s": [], "o": [[], []]}

        def heads(b, n, yq, yk, yv, ev):
            rd = []

            def products4(view, prod, deps):
                held = {}

                def multiply(c):
                    i, big, bf = rHB.take()
                    e = pool if c == 1 else dve
                    if c == 2 or c == 3:
                        e = sooner([deps, bf], (pool, 2.8 + PB), (dve, 1.25 + DB))[0]
                    t3, a, k = prod(big, c)
                    held[c] = (i, t3, op(e, lambda q, t3=t3, a=a, k=k: q.tensor_tensor(t3, a, k, ALU.mult), deps, bf,
                                         c=2.8 if e is pool else 1.25))

                def add(c):
                    i, t3, m = held[c]
                    v = op(dve, lambda q, t3=t3, c=c: q.tensor_reduce(view[:, 4 * c:4 * c + 4, :], t3, AX.X, ALU.add), m, hs_dep[0], c=1.25)
                    rHB.free[i] = [v]
                    return v, m

                multiply(1)
                multiply(0)
                out = [add(0)]
                multiply(3)
                yield "free"
                multiply(2)
                for c in (2, 1, 3):
                    yield "free"
                    out.append(add(c))
                hs_out[0] = out

            def prod1(big, c):
                return (big.rearrange("p (h k d) -> p h k d", h=4, d=HD), yq[:, 4 * c:4 * c + 4, :].unsqueeze(2).broadcast_to([128, 4, NH, HD]),
                        yk.unsqueeze(1).broadcast_to([128, 4, NH, HD]))

            def prod2(big, c):
                return (big.rearrange("p (h d k) -> p h d k", h=4, d=HD), SC[:, 4 * c:4 * c + 4, :].unsqueeze(2).broadcast_to([128, 4, HD, NH]),
                        yv.rearrange("p k d -> p d k").unsqueeze(1).broadcast_to([128, 4, HD, NH]))

            hs_dep, hs_out = [hs_free["s"]], [None]
            yield from products4(SC, prod1, ev)
            dv, rd = [v for v, _ in hs_out[0]], [m for _, m in hs_out[0]]
            yield "free"
            r = op(dve, lambda q: q.tensor_reduce(SM[:, 0:NH], SC, AX.X, ALU.max), dv)
            r = op(dve, lambda q: q.tensor_tensor(SC, SC, SM[:, 0:NH].unsqueeze(2).broadcast_to([128, NH, NH]), ALU.subtract), r)
            yield [r]
            tables("exp")
            x = op(act, lambda q: q.activation(SC, SC, ACT.Exp), r)
            yield [x]
            r = op(dve, lambda q: q.tensor_reduce(SM[:, 0:NH], SC, AX.X, ALU.add), x)
            r = op(dve, lambda q: q.reciprocal(SM[:, NH:2 * NH], SM[:, 0:NH]), r)
            yield
            o = ON[:, :, :, :].rearrange("p a b c -> p (a b c)")[:, n * C:(n + 1) * C].rearrange("p (h d) -> p h d", d=HD)
            hs_dep[0] = hs_free["o"][n]
            yield from products4(o, prod2, [x, ev])
            ov, mu = [v for v, _ in hs_out[0]], [m for _, m in hs_out[0]]
            yield "free"
            v = op(dve, lambda q, o=o: q.tensor_tensor(o, o, SM[:, NH:2 * NH].unsqueeze(2).broadcast_to([128, NH, HD]), ALU.mult), ov, r)
            hs_free["s"] = [v, mu]
            t = d_ho[n].go(sp, scr_o[b, :, n * 128:(n + 1) * 128, :].rearrange("h t d -> t h d"), o, v)
            hs_free["o"][n] = [t]
            tok["ho", b, n] = t
            tok["hd"] = [rd, mu]
            yield

        def middle(b):
            for n in range(2):
                while ("y", b, n) not in tok or "across" not in flags:
                    yield "wait"
                iy, y, ev = tok["y", b, n]
                yq, yk, yv = (y[:, s * C:(s + 1) * C].rearrange("p (h d) -> p h d", d=HD) for s in range(3))
                yield from heads(b, n, yq, yk, yv, ev)
                rY.free[iy] = tok["hd"]
            yield from regroup(1, b)

        def regroup(L, b):
            u = b % 2
            tok["ad", b] = d_ae[u].go(sp, AD2[u], scr_ada[L, b, 2 * C:5 * C].partition_broadcast(128), ae_rd[u], tok[("ada", L), 4])
            src = scr_o[b].rearrange("h t d -> (h t d)").rearrange("(n p c) -> p n c", p=128, c=C)
            tok["o", b] = [d_yo.go(sp, YO, src, yo_rd[0], tok["ho", b, 0], tok["ho", b, 1])]
            yield

        def attend(L, b):
            u = b % 2
            tok["ad", b] = d_ae[u].go(sp, AD2[u], scr_ada[L, b, 2 * C:5 * C].partition_broadcast(128), ae_rd[u], tok[("ada", L), 4])
            og = {}
            red, rec = [], []

            def av(c, s, ready):
                if c % 2 == 0:
                    og["s"] = rO.take()
                j, ps, pf = og["s"]
                for par in range(2):
                    h = 2 * c + par
                    for n in range(2):
                        at = (n * 4 + (h % 4)) * 37
                        big, small = ps[:, at:at + 37], ps[:, at:at + 19]
                        items = [(big, PHI[s][:, kt, par, n * 128:(n + 1) * 128], VB[u][:, kt, h, :]) for kt in range(2)]
                        items += [(small, PLO[s][:, kt, par, n * 128:(n + 1) * 128], VB[u][:, kt, h, 0:19]) for kt in range(2)]
                        m = mms(items, ready, pf, tok["v", b], t_vb)
                rE.free[s] = [m] + [ready]
                if c % 2 == 1:
                    g = c // 2
                    o8 = ps[:, 0:296].rearrange("p (g x) -> p g x", x=37)
                    r = op(dve, lambda q, o8=o8, g=g: q.reciprocal(DN[:, g, :], o8[:, :, 18]), m, dn_rd[0], c=0.1)
                    pair = bass.AP(ps.tensor, ps.offset, [list(ps.ap[0]), [37, 8], [1, 18], [19, 2]])
                    v = op(dve, lambda q, pair=pair, g=g: q.tensor_reduce(
                        ON[:, g, :, :].rearrange("p n (h d) -> p (n h) d", d=HD), pair, AX.X, ALU.add), m, on_rd[0])
                    rO.free[j] = [r, v]
                    red.append(v)
                    rec.append(r)
                return m

            late = []

            def exps():
                i, ps, m, s, half, ef = late.pop(0)
                tables("exp")
                a1 = op(act, lambda q: q.activation(E32[s][:, half], ps, ACT.Exp), m, ef, c=0.63)
                a2 = op(act, lambda q: q.activation(PHI[s].rearrange("p k a t -> p (k a t)")[:, half], ps, ACT.Exp), m, ef, c=0.63)
                rA.free[i] = [a1, a2]
                return [a1, a2]

            def low(s, got, ef):
                hi = PHI[s].rearrange("p k a t -> p (k a t)")
                lo = PLO[s].rearrange("p k a t -> p (k a t)")
                at = eta([got, ef])
                z = min(ZS, key=lambda z: max(max(dve.clock, at) + 0.08 + z * 0.00115, max(pool.clock, at) + (1024 - z) * 0.002))
                d = op(dve, lambda q: q.tensor_tensor(lo[:, 0:z], E32[s][:, 0:z], hi[:, 0:z], ALU.subtract), got, ef, c=0.08 + z * 0.00115)
                p = op(pool, lambda q: q.tensor_tensor(lo[:, z:1024], E32[s][:, z:1024], hi[:, z:1024], ALU.subtract), got, ef, c=(1024 - z) * 0.002)
                return [got, d, p]

            def scores(c, kt, s, ef):
                i, ps, pf = rA.take()
                for par in range(2):
                    m = mms([(ps[:, par * 256:(par + 1) * 256], KZ[u][:, c, par, kt * 128:(kt + 1) * 128], QT[u][:, c, :])],
                            tok["qk", b], pf, t_kz)
                late.append((i, ps, m, s, slice(kt * 512, kt * 512 + 512), ef))
                return m

            last_e, last_s = None, None
            for c in range(8):
                s, _, ef = rE.take()
                m = scores(c, 0, s, ef)
                if c:
                    e1 = exps()
                    yield [e1]
                    ready = low(last_s[0], [last_e, e1], last_s[1])
                else:
                    yield [m]
                last_e = exps()
                m = scores(c, 1, s, ef)
                yield [last_e]
                if c:
                    m2 = av(c - 1, last_s[0], ready)
                last_s = (s, ef)
                yield [last_e]
            e1 = exps()
            yield [e1]
            ready = low(last_s[0], [last_e, e1], last_s[1])
            yield [ready]
            m2 = av(7, last_s[0], ready)
            qt_rd[u], kz_rd[u], vb_rd[u] = [m], [m], [m2]
            yield [m2]
            outs = []
            for n in range(2):
                o3 = YO[:, n, :].rearrange("p (g h d) -> p g h d", g=4, d=HD)
                i3 = ON[:, :, n, :].rearrange("p g (h d) -> p g h d", d=HD)
                r3 = DN[:, :, n * 4:n * 4 + 4].unsqueeze(3).broadcast_to([128, 4, 4, HD])
                outs.append(op(dve, lambda q, o3=o3, i3=i3, r3=r3: q.tensor_tensor(o3, i3, r3, ALU.mult), red, rec, yo_rd[0]))
            on_rd[0] = dn_rd[0] = outs
            tok["o", b] = outs
            yield

        def finish(L, b):
            u = b % 2
            g1 = AD2[u][:, 0:C]
            adt = tok["ad", b]
            yield from to_columns(1, b, YO, tok["o", b])
            yo_rd[0] = tok["read"]
            for n in range(2):
                t = 2 * b + n
                yield from slot(rC)
                j, ps, pf = rC.take()
                o = ps[:, 0:C]
                m = mms(products(o, lambda x: XT[:, x, t * 128:(t + 1) * 128], lambda w: WP[:, w, :]), TW[t], tok["wp", L], pf)
                TR[t] = [m]
                wp_rd[0] = [m]
                yield [m]
                k, tm, tf = rTM.take()
                v = op(dve, lambda q, o=o, tm=tm: q.scalar_tensor_tensor(
                    out=tm, in0=o, scalar=1.0 / WS, in1=g1, op0=ALU.mult, op1=ALU.mult), m, adt, tf)
                rC.free[j] = [v]
                p = op(pool, lambda q, t=t, tm=tm: q.tensor_tensor(X[:, t, :], X[:, t, :], tm, ALU.add), v, XW[t], XR[t])
                rTM.free[k] = [p]
                XW[t], XR[t] = [p], []
                yield "free" if n == 0 else None
            yield from layernorm(1, b, AD2[u][:, 2 * C:3 * C], AD2[u][:, C:2 * C], adt)
            ae_rd[u] = [tok["lnd"], v]
            if L == 0:
                for n in range(2):
                    t = 2 * b + n
                    yield from slot(rC)
                    j, ps, pf = rC.take()
                    o = ps[:, 0:NE]
                    m = mms(products(o, lambda x: XT[:, x, t * 128:(t + 1) * 128], lambda w: WG[:, w, :]), TW[t], tok["wg"], pf)
                    yield [m]
                    v = op(dve, lambda q, o=o, t=t: q.tensor_scalar(LG[:, t, :], o, 1.0 / WS, None, ALU.mult), m)
                    rC.free[j] = [v]
                    tok["lg", t] = v
                yield
            if b % 2:
                ms.ready.add((L, b // 2))

        def gates(c4):
            lg = [tok["lg", t] for t in range(4 * c4, 4 * c4 + 4)]
            l3, CW, CWS = (z[:, 4 * c4:4 * c4 + 4, :] for z in (LG, CWA, CWSA))
            before = tok.get("cw", [])
            a = op(dve, lambda q: q.tensor_reduce(L1[:, :], l3, AX.X, ALU.max), lg, before)
            b = op(dve, lambda q: q.tensor_tensor(CW, l3, L1[:, :].unsqueeze(2).broadcast_to([128, 4, NE]), ALU.subtract), a)
            c = op(act, lambda q: q.activation(CW, CW, ACT.Exp), b)
            e4 = l3.unsqueeze(3).broadcast_to([128, 4, NE, NE])
            j4 = l3.unsqueeze(2).broadcast_to([128, 4, NE, NE])
            t4 = LT[:, :, :].rearrange("p t (e j) -> p t e j", e=NE)
            m4 = LM[:, :, :].rearrange("p t (e j) -> p t e j", e=NE)
            d = op(dve, lambda q: q.tensor_tensor(t4, j4, e4, ALU.is_gt), lg, before)
            e = op(dve, lambda q: q.tensor_tensor(m4, j4, e4, ALU.is_equal), lg, before)
            e = op(dve, lambda q: q.tensor_tensor(LM[:, :, :], LM[:, :, :], TRI[:, :].unsqueeze(1).broadcast_to([128, 4, 16]), ALU.mult), e, t_tri)
            e = op(dve, lambda q: q.tensor_tensor(LT[:, :, :], LT[:, :, :], LM[:, :, :], ALU.add), e, d)
            e = op(dve, lambda q: q.tensor_reduce(CWS, t4, AX.X, ALU.add), e)
            e = op(dve, lambda q: q.tensor_scalar(CWS, CWS, 1.5, None, ALU.is_lt), e)
            f = op(dve, lambda q: q.tensor_tensor(CW, CW, CWS, ALU.mult), e, c)
            g = op(dve, lambda q: q.tensor_reduce(L1[:, :], CW, AX.X, ALU.add), f)
            g = op(dve, lambda q: q.reciprocal(L1[:, :], L1[:, :]), g)
            g = op(dve, lambda q: q.tensor_tensor(CW, CW, L1[:, :].unsqueeze(2).broadcast_to([128, 4, NE]), ALU.mult), g, f)
            h = op(dve, lambda q: q.tensor_scalar(CWS, CW, 1.0 / WS, None, ALU.mult), g)
            tok["cw"] = [g, h]

        g2_rd, h_rd, hw = [[]], [[]], {}

        def up(L, e, c):
            fn_act = LW[L]["act"]
            done = []
            xt = [TW[t] for t in range(4 * c, 4 * c + 4)]
            acts, lows = [], []

            def activate():
                m, i, ps, mt = acts.pop(0)
                tables("gelu")
                gi, g, gf = rG.take()
                hi = H[:, m, 0, :]
                a1 = op(act, lambda q: q.activation(g, ps, fn_act, scale=1.0 / WS), mt, gf, c=0.63)
                a2 = op(act, lambda q: q.activation(hi, ps, fn_act, scale=1.0 / WS), mt, h_rd[0], c=0.63)
                rU.free[i] = [a1, a2]
                lows.append((m, gi, g, a1, a2))
                return [a1, a2]

            def low():
                m, gi, g, a1, a2 = lows.pop(0)
                e, c = sooner([a1, a2], (pool, 1.25 + PB), (dve, 0.6))
                d = op(e, lambda q: q.tensor_tensor(H[:, m, 1, :], g, H[:, m, 0, :], ALU.subtract), a1, a2, h_rd[0], c=c)
                rG.free[gi] = [d]
                done.extend([a2, d])

            for m in range(9):
                yield from slot(rU)
                i, ps, pf = rU.take()
                mt = mms(products(ps, lambda w: W1[:, w, m * 128:(m + 1) * 128],
                                  lambda x: XT[:, x, c * 512:(c + 1) * 512], swap=True), tok["w1"], xt, pf)
                if lows:
                    low()
                if acts:
                    activate()
                acts.append((m, i, ps, mt))
                yield "free"
            low()
            activate()
            yield "free"
            low()
            w1_rd[0] = [w1_rd[0], mt] if (1, e) in saved and L == 0 else [mt]
            for t in range(4 * c, 4 * c + 4):
                TR[t] = TR[t] + [mt]
            hw["now"] = done

        def down(L, e, c):
            ht = hw["now"]
            for n in range(4):
                t = 4 * c + n
                yield from slot(rU)
                i, ps, pf = rU.take()
                o = ps[:, 0:C]
                items = [(o, ONES[:, :], W2[:, 18, :])]
                for m in range(9):
                    hi, lo = (H[:, m, s, n * 128:(n + 1) * 128] for s in range(2))
                    items += [(o, hi, W2[:, 2 * m, :]), (o, hi, W2[:, 2 * m + 1, :]), (o, lo, W2[:, 2 * m, :])]
                for k in range(28):
                    fn = lambda q, it=items[k], k=k: q.matmul(*it, start=(k == 0), stop=(k == 27))
                    if k == 27:
                        mt = op(pe, fn, c=0.15)
                    else:
                        quiet(pe, fn, [ht, tok["w2"], pf, t_on] if k == 0 else [], c=0.15)
                    if k == 9 or k == 18:
                        yield "free"
                yield [mt]
                k, tm, tf = rTM.take()
                scal = CWSA[:, t, e:e + 1] if L == 0 else 1.0 / WS
                g = G2[:, n // 2, :]
                v = op(dve, lambda q, o=o, tm=tm, scal=scal, g=g: q.scalar_tensor_tensor(
                    out=tm, in0=o, scalar=scal, in1=g, op0=ALU.mult, op1=ALU.mult), mt, tok["g2"], tf, tok["cw"] if L == 0 else [])
                rU.free[i] = [v]
                v2 = op(pool, lambda q, t=t, tm=tm: q.tensor_tensor(X[:, t, :], X[:, t, :], tm, ALU.add), v, XW[t], XR[t])
                rTM.free[k] = [v2]
                XW[t], XR[t] = [v2], []
                if n % 2 and (len(ms.todo) < 2 or ms.todo[1][0::2] != (L, c)):
                    flags.add(("x", L, t // 2))
            h_rd[0] = [mt]
            w2_rd[0] = [w2_rd[0], mt] if (2, e) in saved and L == 0 else [mt]
            g2_rd[0] = [v]

        def skew():
            run_v = cond_done_v[0]
            z = op(pool, lambda q: q.memset(EX[:, :, :, :], 0.0))
            v4 = scr_v.rearrange("(q h) n -> h q n", h=2)
            for hf in range(2):
                src = v4[hf, :, 0:2048].rearrange("q (i j) -> i q j", j=D)
                t = d_v.go(sp, EX[64 * hf:64 * hf + 32, :, 0, :], src, z, run_v)
                src = v4[hf, :, 2048:3072].rearrange("q (i j) -> i q j", j=32)
                t = d_v.go(sp, EX[64 * hf + 32:64 * hf + 64, :, 0, 32:64], src)
                yield
            tok["vrd"] = [t, z]
            yield

        def expm_steps():
            t, z = tok["vrd"]

            def pairs(ps, kinds, lhs, rhs, *deps):
                n = 0
                for q4 in range(4):
                    for hf in range(2):
                        sl = slice(64 * hf, 64 * hf + 64)
                        for kd in range(kinds):
                            m = mms([(ps[sl, q4, kd, :], lhs(sl, q4, kd), rhs(sl, q4, kd))], deps)
                return m

            def bank():
                j, ps, pf = rC.take()
                return j, ps.rearrange("p (q k n) -> p q k n", q=4, k=2), pf

            s = 2.0 ** -NSQ
            yield from slot(rC)
            j, ps, pf = bank()
            m = pairs(ps, 1, lambda sl, a, k: EX[sl, a, 0, :], lambda sl, a, k: ID2[sl, :], t, z, t_id2, pf)
            v = op(dve, lambda q: q.tensor_tensor(EY[:, :, 1, :], ps[:, :, 0, :], EX[:, :, 0, :], ALU.subtract), m, t, z)
            rC.free[j] = [v]
            a = op(dve, lambda q: q.tensor_scalar(EX[:, :, 0, :], EY[:, :, 1, :], -s, None, ALU.mult), v, m)
            a2 = op(dve, lambda q: q.tensor_scalar(EX[:, :, 1, :], EY[:, :, 1, :], s, None, ALU.mult), v, m)
            yield
            yield from slot(rC)
            j, p1, pf = bank()
            m = pairs(p1, 1, lambda sl, a, k: EX[sl, a, 1, :], lambda sl, a, k: EX[sl, a, 0, :], a, a2, pf)
            y1 = op(dve, lambda q: q.tensor_copy(EY[:, :, 0, :], p1[:, :, 0, :]), m, a, a2)
            rC.free[j] = [y1]
            yield
            yield from slot(rC)
            j, p2, pf = bank()
            m = pairs(p2, 1, lambda sl, a, k: EY[sl, a, 0, :], lambda sl, a, k: EY[sl, a, 0, :], y1, pf)
            y2 = op(dve, lambda q: q.tensor_copy(EY[:, :, 1, :], p2[:, :, 0, :]), m, y1)
            rC.free[j] = [y2]
            yield
            yield from slot(rC)
            j, p3, pf = bank()
            m = pairs(p3, 2, lambda sl, a, k: EY[sl, a, 1, :], lambda sl, a, k: EY[sl, a, k, :], y2, y1, pf)
            Cc, Gg = EW[:, :, 0, :], EW[:, :, 1, :]
            idb = ID2[:, :].unsqueeze(1).broadcast_to([128, 4, D])
            c1 = op(dve, lambda q: q.tensor_scalar(Cc, EY[:, :, 0, :], 0.5, None, ALU.mult), y1)
            g1 = op(dve, lambda q: q.scalar_tensor_tensor(out=Gg, in0=EY[:, :, 0, :], scalar=1.0 / 6, in1=idb, op0=ALU.mult, op1=ALU.add), y1, t_id2)
            for src, fc, fg, dp in ((EY[:, :, 1, :], 1.0 / 24, 1.0 / 120, y2), (p3[:, :, 0, :], 1.0 / 720, 1.0 / 5040, m),
                                    (p3[:, :, 1, :], 1.0 / 40320, 1.0 / 362880, m)):
                c1 = op(dve, lambda q, src=src, fc=fc: q.scalar_tensor_tensor(out=Cc, in0=src, scalar=fc, in1=Cc, op0=ALU.mult, op1=ALU.add), c1, dp)
                g1 = op(dve, lambda q, src=src, fg=fg: q.scalar_tensor_tensor(out=Gg, in0=src, scalar=fg, in1=Gg, op0=ALU.mult, op1=ALU.add), g1, dp)
            rC.free[j] = [c1, g1]
            yield
            yield from slot(rC)
            j, p5, pf = bank()
            m = pairs(p5, 1, lambda sl, a, k: EX[sl, a, 1, :], lambda sl, a, k: EW[sl, a, 1, :], g1, pf)
            e1 = op(dve, lambda q: q.tensor_tensor(EY[:, :, 0, :], p5[:, :, 0, :], Cc, ALU.add), m, c1)
            e2 = op(dve, lambda q: q.scalar_tensor_tensor(out=EY[:, :, 1, :], in0=p5[:, :, 0, :], scalar=-1.0, in1=Cc, op0=ALU.mult, op1=ALU.add), m, c1)
            rC.free[j] = [e1, e2]
            dn = [e1, e2, m]
            yield
            cur, oth = EY, EX
            for _ in range(NSQ):
                yield from slot(rC)
                j, p6, pf = bank()
                m = pairs(p6, 2, lambda sl, a, k: cur[sl, a, 1 - k, :], lambda sl, a, k: cur[sl, a, k, :], dn, pf)
                dn = [op(dve, lambda q, o=oth, c=cur, p6=p6: q.scalar_tensor_tensor(
                    out=o[:, :, :, :].rearrange("p a b c -> p (a b c)"), in0=c[:, :, :, :].rearrange("p a b c -> p (a b c)"), scalar=2.0,
                    in1=p6.rearrange("p a b c -> p (a b c)"), op0=ALU.mult, op1=ALU.add), m, dn)]
                rC.free[j] = dn
                dn = dn + [m]
                cur, oth = oth, cur
                yield
            tok["E"] = (cur, dn)

        def householder():
            at = [t_at]
            nb, sg, g, rt, w, d = (HS[:, k:k + 1] for k in range(6))
            hs, n2t = [], []
            hp = sb("HP", [D, 1])
            t_hp = op(pool, lambda q: q.memset(hp[:, :], 0.5))
            sqw = []
            yield
            for j in range(D):
                yield from slot(rU)
                c, ps, pf = rU.take()
                bc = ps[0:D, 0:C - j]
                aj = AT[:, j:C]
                m = mms([(bc, IDF[0:D, j:j + 1].broadcast_to([D, D]), aj)], at, t_idf, pf)
                yield
                m = op(act, lambda q, bc=bc, j=j: q.activation(BC[:, j:C], bc, ACT.Copy), m, hs, sqw, c=0.4)
                rU.free[c] = [m]
                bc = BC[:, j:C]
                s1 = op(act, lambda q, bc=bc, j=j: q.activation(sq[:, j:C], bc, ACT.Square, accum_out=N2[:, 0:1]), m, n2t, sqw, c=0.4)
                yield
                s2 = tiny(dve, lambda q, bc=bc, aj=aj, j=j: q.tensor_tensor_reduce(
                    out=HQ[:, j:C], in0=bc, in1=aj, scale=1.0, scalar=0.0, op0=ALU.mult, op1=ALU.add, accum_out=d), m, s1, at, hs)
                p = tiny(pool, lambda q: q.tensor_tensor(N2[:, 1:2], N2[:, 0:1], hp[:, :], ALU.pow), s1, t_hp, n2t)
                a = tiny(dve, lambda q, bc=bc: q.tensor_scalar(sg, bc[:, 0:1], 0.0, 2.0, ALU.is_ge, ALU.mult), m, s1, hs)
                b = tiny(dve, lambda q: q.scalar_tensor_tensor(out=nb, in0=sg, scalar=1.0, in1=N2[:, 1:2], op0=ALU.subtract, op1=ALU.mult), a, p, hs)
                e = tiny(dve, lambda q, bc=bc, j=j: q.scalar_tensor_tensor(out=TI[:, j:j + 1], in0=nb, scalar=bc[:, 0:1], in1=N2[:, 0:1], op0=ALU.mult, op1=ALU.add), b, s1)
                r = tiny(dve, lambda q, j=j: q.reciprocal(rt, TI[:, j:j + 1]), e, hs)
                f = tiny(dve, lambda q, j=j: q.scalar_tensor_tensor(out=w, in0=AT[:, j:j + 1], scalar=nb, in1=d, op0=ALU.mult, op1=ALU.add), b, s2, hs, at)
                g1 = tiny(dve, lambda q, j=j: q.scalar_tensor_tensor(out=g, in0=w, scalar=rt, in1=NMK[:, j:j + 1], op0=ALU.mult, op1=ALU.mult), f, r, t_nmk, hs)
                x = tiny(dve, lambda q, bc=bc, aj=aj: q.scalar_tensor_tensor(out=aj, in0=bc, scalar=g, in1=aj, op0=ALU.mult, op1=ALU.add), g1, m, s2)
                y = tiny(dve, lambda q, j=j: q.scalar_tensor_tensor(out=AT[:, j:j + 1], in0=g, scalar=nb, in1=AT[:, j:j + 1], op0=ALU.mult, op1=ALU.add), x)
                y = tiny(dve, lambda q, j=j: q.scalar_tensor_tensor(out=AT[:, j:j + 1], in0=IDF[0:D, j:j + 1], scalar=nb, in1=AT[:, j:j + 1], op0=ALU.mult, op1=ALU.add), y, t_idf)
                at = [x, y]
                hs = [y]
                n2t = [y, p]
                sqw = [s1]
                yield
            v0 = op(pool, lambda q: q.memset(UT[0:D, :], 0.0))
            cp = op(dve, lambda q: q.tensor_tensor(UT[0:D, 0:D], AT[:, 0:D], MGE[:, :], ALU.mult), at, v0, t_m)
            cp2 = op(dve, lambda q: q.tensor_copy(UT[0:D, D:C], AT[:, D:C]), at, v0)
            VT = UT[0:D, :]
            vt = [cp, cp2]
            yield from slot(rC)
            j, ps, pf = rC.take()
            for k in range(3):
                m = op(pe, lambda q, k=k, ps=ps: q.transpose(ps[0:96, k * D:(k + 1) * D], VT[:, k * 96:(k + 1) * 96], IDF[0:D, 0:D]), vt, pf, t_idf)
            VR = STGV[:, 0:3 * D].rearrange("p (k n) -> p k n", k=3)
            c1 = op(dve, lambda q, ps=ps: q.tensor_copy(VR, ps[0:96, 0:3 * D].rearrange("p (k n) -> p k n", k=3)), m, cond_done_v[0])
            rC.free[j] = [c1]
            yield
            yield from slot(rC)
            j, ps, pf = rC.take()
            m = mms([(ps[0:D, 0:D], VR[:, k, :], VR[:, k, :]) for k in range(3)], c1, pf)
            dg = HS[:, 6:7]
            di = HS[:, 7:8]
            q1 = op(dve, lambda q: q.tensor_tensor_reduce(out=NN[:, 0, :], in0=TI[:, :], in1=IDF[0:D, 0:D], scale=1.0, scalar=0.0,
                                                          op0=ALU.mult, op1=ALU.add, accum_out=dg), at)
            q2 = op(dve, lambda q: q.reciprocal(di, dg), q1)
            q3 = op(dve, lambda q, ps=ps: q.scalar_tensor_tensor(out=NN[:, 0, :], in0=ps[0:D, 0:D], scalar=di, in1=MLT[:, :], op0=ALU.mult, op1=ALU.mult), q2, m)
            rC.free[j] = [q3]
            yield
            yield from slot(rC)
            j, ps, pf = rC.take()
            m = op(pe, lambda q, ps=ps: q.transpose(ps[0:D, 0:D], NN[:, 0, :], IDF[0:D, 0:D]), q3, pf)
            nt = op(dve, lambda q, ps=ps: q.tensor_copy(NN[:, 1, :], ps[0:D, 0:D]), m)
            pt = op(dve, lambda q, ps=ps: q.scalar_tensor_tensor(out=NP[:, 0, :], in0=ps[0:D, 0:D], scalar=-1.0, in1=IDF[0:D, 0:D], op0=ALU.mult, op1=ALU.add), m)
            rC.free[j] = [nt, pt]
            cur = 0
            nn = [q3, nt]
            prd = []
            yield
            for k in range(5):
                yield from slot(rC)
                j, ps, pf = rC.take()
                m1 = mms([(ps[0:D, 0:D], NN[:, 2 * cur + 1, :], NN[:, 2 * cur, :])], nn, pf)
                m1 = mms([(ps[0:D, D:2 * D], NN[:, 2 * cur, :], NN[:, 2 * cur + 1, :])])
                nx = 1 - cur
                c2 = op(dve, lambda q, ps=ps, nx=nx: q.tensor_copy(NN[:, 2 * nx:2 * nx + 2, :].rearrange("p a b -> p (a b)"), ps[0:D, 0:2 * D]), m1, nn, prd)
                rC.free[j] = [c2]
                yield
                yield from slot(rC)
                j, ps, pf = rC.take()
                m2 = mms([(ps[0:D, 0:D], NN[:, 2 * nx, :], NP[:, 0, :])], c2, pt, pf)
                pt = op(dve, lambda q, ps=ps: q.tensor_tensor(NP[:, 0, :], ps[0:D, 0:D], NP[:, 0, :], ALU.add), m2, pt)
                rC.free[j] = [pt]
                prd = [m2]
                nn = [c2]
                cur = nx
                yield
            yield from slot(rC)
            j, ps, pf = rC.take()
            m = op(pe, lambda q, ps=ps: q.transpose(ps[0:D, 0:D], NP[:, 0, :], IDF[0:D, 0:D]), pt, pf)
            pp = op(dve, lambda q, ps=ps: q.tensor_copy(NP[:, 1, :], ps[0:D, 0:D]), m)
            rC.free[j] = [pp]
            yield
            yield from slot(rC)
            j, ps, pf = rC.take()
            m = mms([(ps[0:D, 0:C], NP[:, 1, :], VT)], pp, vt, pf)
            zz = op(dve, lambda q, ps=ps: q.tensor_scalar(AT[:, :], ps[0:D, 0:C], di, None, ALU.mult), m, q2, at, c1)
            rC.free[j] = [zz]
            yield
            yield from slot(rC)
            j, ps, pf = rC.take()
            m = mms([(ps[0:D, 0:C], VT[:, 0:D], AT[:, :])], zz, pf)
            u1 = op(dve, lambda q, ps=ps: q.tensor_tensor(UT[0:D, 0:D], IDF[0:D, 0:D], ps[0:D, 0:D], ALU.subtract), m)
            u2 = op(dve, lambda q, ps=ps: q.tensor_scalar(UT[0:D, D:C], ps[0:D, D:C], -1.0, None, ALU.mult), m)
            rC.free[j] = [u1, u2]
            yield
            t = d_p.go(sp, UT[D:2 * D, :], UT[0:D, :], u1, u2)
            rep = op(dve, lambda q: q.tensor_copy(NP[:, :, :].rearrange("p a b -> p (a b)").rearrange("p (r c) -> p r c", r=4),
                                                  UT[0:D, 256:C].unsqueeze(1).broadcast_to([D, 4, 32])), u2, m, pp)
            yield from slot(rC)
            j, ps, pf = rC.take()
            for k in range(3):
                src = UT[0:D, k * 128:(k + 1) * 128] if k < 2 else NP[:, :, :].rearrange("p a b -> p (a b)")
                m = op(pe, lambda q, k=k, ps=ps, src=src: q.transpose(ps[:, k * D:(k + 1) * D], src, IDF[0:D, 0:D]), u1, u2, rep, pf)
            p3 = ps[:, 0:3 * D].rearrange("p (k n) -> p k n", k=3)
            h = op(act, lambda q, p3=p3: q.activation(WU[:, 0:3, :], p3, ACT.Copy, scale=WS), m)
            l1 = op(dve, lambda q, p3=p3: q.scalar_tensor_tensor(out=WU[:, 3:5, :], in0=p3[:, 0:2, :], scalar=WS, in1=WU[:, 0:2, :], op0=ALU.mult, op1=ALU.subtract), h)
            l2 = op(dve, lambda q, p3=p3: q.scalar_tensor_tensor(out=WU[64:128, 2, :], in0=p3[64:128, 2, :], scalar=WS, in1=WU[64:128, 2, :], op0=ALU.mult, op1=ALU.subtract), h)
            rC.free[j] = [h, l1, l2]
            zu = op(dve, lambda q: q.memset(WU[96:128, 2, :], 0.0), h, l2)
            tok["U"] = [h, l1, l2, t, u1, u2, zu]
            yield

        HQS = sb("HQS", [D, 3 * C])
        HQ, sq, BC = (HQS[:, k * C:(k + 1) * C] for k in range(3))
        NN = OSM[0:D, 0:4 * D].rearrange("p (a b) -> p a b", b=D)
        NP = OSM[0:D, 4 * D:6 * D].rearrange("p (a b) -> p a b", b=D)
        STGV = OSM[0:96, 6 * D:9 * D]
        MGE = sb("MGE", [D, D])
        MLT = sb("MLT", [D, D])
        k1 = op(pool, lambda q: q.memset(MGE[:, :], 1.0))
        k2 = op(pool, lambda q: q.memset(MLT[:, :], 0.0))
        op(pool, lambda q: q.affine_select(out=MGE[:, :], in_=MGE[:, :], compare_op=ALU.is_ge, fill=0.0,
                                           base=0, pattern=[[1, D]], channel_multiplier=-1), k1, k2)
        t_m = op(pool, lambda q: q.affine_select(out=MLT[:, :], in_=MLT[:, :], compare_op=ALU.is_ge, fill=1.0,
                                                 base=0, pattern=[[-1, D]], channel_multiplier=1), k1, k2)

        def last_buffers(fence):
            used = arena[0:D, 0:8192].bitcast(F32)
            rZ = Ring([used[:, i * 256:(i + 1) * 256] for i in range(2)])
            rM = Ring([used[:, 512 + i * C:512 + (i + 1) * C] for i in range(2)])
            rOut = Ring([arena[:, 2304 + 1152 * i:3456 + 1152 * i].bitcast(F32).rearrange("p (a c) -> p a c", c=C) for i in range(2)])
            for r in (rZ, rM, rOut):
                r.free = [[fence], [fence]]
            return rZ, rM, rOut

        def rotated(rings, first):
            rZ, rM, rOut = rings
            cur, et = tok["E"]
            o_v = out.rearrange("(t p) c -> p t c", p=128)
            for b in range(first, B, 2):
                yield from ms.wait(2, b)
                sl = slice(64 * (b % 2), 64 * (b % 2) + 64)
                yield from slot(rC)
                j, ps, pf = rC.take()
                m = mms([(ps[0:D, 0:C], cur[sl, b // 2, 1, :], UT[sl, :])], et, tok["U"], pf)
                yield [m]
                im, mb, mf = rM.take()
                mbt = op(act, lambda q, ps=ps, mb=mb: q.activation(mb, ps[0:D, 0:C], ACT.Copy), m, mf)
                rC.free[j] = [mbt]
                xw = [XW[2 * b], XW[2 * b + 1]]
                yield from to_columns(b % 2, b, X[:, 2 * b:2 * b + 2, :], xw)
                yield from slot(rC)
                j, ps, pf = rC.take()
                m = mms(products(ps[0:D, 0:256], lambda w: WU[:, w, :], lambda x: XT[:, x, b * 256:(b + 1) * 256], swap=True),
                        TW[2 * b], TW[2 * b + 1], tok["U"], pf)
                yield [m]
                iz, z, zf = rZ.take()
                a = op(act, lambda q, z=z, ps=ps: q.activation(z, ps[0:D, 0:256], ACT.Copy, scale=1.0 / WS), m, zf)
                rC.free[j] = [a]
                yield
                io, o, of = rOut.take()
                ds = []
                for n in range(2):
                    yield from slot(rC)
                    j, ps, pf = rC.take()
                    m = mms([(ps[:, 0:C], z[:, n * 128:(n + 1) * 128], mb)], a, mbt, pf)
                    v = op(dve, lambda q, ps=ps, o=o, n=n, b=b: q.tensor_tensor(o[:, n, :], ps[:, 0:C], X[:, 2 * b + n, :], ALU.add), m, xw, of)
                    rC.free[j] = [v]
                    ds.append(v)
                rZ.free[iz] = [m]
                rM.free[im] = [m]
                t = d_out[io].go(sp, o_v[:, 2 * b:2 * b + 2, :], o, ds)
                rOut.free[io] = [t]
                yield

        cond_done_v = [None]

        def ada(L):
            w, b = LW[L]["a"]
            yield from cond_rows(I[w], I[b], 6 * C, scr_ada[L], lambda k: 1.0 if k in (1, 4) else 0.0, ("ada", L))

        def vrows():
            yield from cond_rows(I["L3_WT"], I["L3_bp"], 11 * C, scr_v, lambda k: 0.0)
            cond_done_v[0] = cond_done[-1]

        class Stream:

            def __init__(self):
                self.todo, order = [], [0, 1, 2, 3]
                for L in range(3):
                    for c in range(4):
                        for e in order if L == 0 else [0]:
                            self.todo.append((L, e, c))
                        order = order[::-1]
                self.half, self.ready, self.done = 0, set(), set()
                self.steps = self.side = self.prev = self.now = None

            def able(self):
                return bool(self.todo) and self.todo[0][0::2] in self.ready

            def start(self):
                L, e, c = self.todo[0]
                if self.half == 0:
                    if (L, c, "g") not in self.done:
                        self.done.add((L, c, "g"))
                        tok["g2"] = d_g2.go(sp, G2[:, :, :], scr_ada[L, 2 * c:2 * c + 2, 5 * C:6 * C].partition_broadcast(128), g2_rd[0], tok[("ada", L), 5])
                    need = self.change(-1)
                    side = w2_load(*need) if need else iter(())
                    self.steps, self.side = up(L, e, c), side
                else:
                    if L == 0 and (c, "cw") not in self.done:
                        self.done.add((c, "cw"))
                        gates(c)
                    need = self.change(1)
                    side = w1_load(*need) if need else iter(())
                    self.steps, self.side = down(L, e, c), side

            def change(self, way):
                if way == -1:
                    now, other = self.todo[0], self.prev
                    want = now
                else:
                    now = self.todo[0]
                    other = self.todo[1] if len(self.todo) > 1 else None
                    want = other
                if other is None or now[0:2] == other[0:2]:
                    return None
                return want[0], want[1]

            def piece(self):
                self.start()
                for k, v in enumerate(self.steps):
                    if k % 2 == 0:
                        next(self.side, None)
                    yield v
                run(self.side)
                self.half = 1 - self.half
                if self.half == 0:
                    self.prev = self.todo.pop(0)
                    L, _, c = self.prev
                    if not self.todo or self.todo[0][0::2] != (L, c):
                        self.done.add((L, c))

            def wait(self, L, c):
                while ("x", L, c) not in flags:
                    yield "wait"

            def line(self, half=None):
                if half is not None and half != self.half:
                    return []
                if self.now is not None and not self.now.over:
                    return [self.now]
                if self.able():
                    self.now = Line(self.piece(), RANKS)
                    return [self.now]
                return []

        ms = Stream()

        class Line:

            def __init__(self, gen, rank, after=()):
                self.gen, self.rank, self.when, self.before, self.over = gen, rank, eta(after), 0.0, False
                self.waits = False

            def step(self):
                newest[0] = 0.0
                v = next(self.gen, "end")
                if v == "end":
                    self.over = True
                    return
                self.waits = v == "wait"
                if v == "wait":
                    self.when = max(self.when, pe.clock) + 0.3
                    return
                self.when = self.before if v == "free" else eta(v) if isinstance(v, list) else newest[0]
                self.before = newest[0]

        def deal(need, others=(), stream=False):
            while not all(x.over for x in need):
                lines = [x for x in (*need, *others, *(ms.line() if (stream() if callable(stream) else stream) else ())) if not x.over]
                now = [x for x in lines if x.when <= pe.clock + SLACK]
                best = min(now, key=lambda x: x.rank) if now else min(lines, key=lambda x: x.when)
                best.step()

        bg = Line(iter(()), 5)

        def until(L, c):
            while (L, c) not in ms.done:
                piece = ms.line()
                assert piece
                deal(piece, [bg])

        def attention(L, before, first, after):
            deal([first, *before], [bg], stream=L > 0)
            for b in range(B):
                fin = Line(finish(L, b - 1) if b else iter(()), RF[L], tok["o", b - 1] if b else ())
                nxt = Line(prep(L, b + 1), RP[L]) if b + 1 < B else after
                at = attend(L, b)
                for n in (NP1, 99):
                    if L == 0:
                        deal(ms.line(1), [fin, nxt, bg])
                    deal(ms.line(0), [fin, nxt, bg])
                    deal([Line(part(at, n), RA)], [fin, nxt, bg, *ms.line(1)])
                deal([fin, nxt] if b + 1 < B else [fin], [bg], stream=lambda: b < B - 1 and nxt.waits)

        def across(before, first, after):
            deal([first], [bg, *before], stream=True)
            for b in range(B):
                fin = [Line(finish(1, b - 1), R1F, tok["o", b - 1])] if b else before
                nxt = [Line(prep(1, b + 1), R1N)] if b + 1 < B else []
                deal([*fin, *nxt, Line(middle(b), R1M)], [bg] if b + 1 < B else [bg, after], stream=True)

        rY.free[2] = None

        def retire():
            h_rd[0] = rSTG.free[2:6]
            rSTG.free[2:6] = [None] * 4
            yield

        n0 = ada(0)
        run(part(n0, 4))
        run(wq_load(0))
        bg = Line(chain(n0, wp_load(0), wg_load(), w1_load(0, 0), w2_load(0, 0), retire(), vrows(), ada(1), ada(2), skew(), householder(), expm_steps()), RB)
        first = Line(chain(wq_load(1), prep(1, 0)), 2)
        attention(0, [], Line(prep(0, 0), 2), first)
        f = last()
        rHB.free = [[f] for _ in rHB.items]
        hs_free["s"], hs_free["o"] = [f], [[f], [f]]
        end = Line(chain(finish(0, B - 1), wp_load(1)), 1, tok["o", B - 1])
        if stop == 0:
            deal([end])
            until(0, 3)
        else:
            flags.add("across")
            rY.free[2] = [f]

            def ahead():
                while ("q", B - 1) not in flags:
                    yield "wait"
                yield from wq_load(2)
                yield from prep(2, 0)

            after = Line(ahead(), 2.5)
            across([end], first, after)
            f = last()
            rE.free = [[f], [f]]
            qt_rd[1] = [f]
            on_rd[0] = dn_rd[0] = [f, hs_free["o"]]
            end = Line(chain(finish(1, B - 1), wp_load(2)), 1, tok["o", B - 1])
            if stop == 1:
                deal([end])
                until(1, 3)
            else:
                attention(2, [end], after, Line(iter(()), 2))
                deal([Line(finish(2, B - 1), 1, tok["o", B - 1])], [bg], stream=True)
                if stop == 2:
                    until(2, 3)
        f = last()
        if stop is None:
            deal([bg])
            rings = last_buffers(f)
            deal([Line(rotated(rings, k), 1) for k in range(2)], stream=True)
        else:
            o_v = out.rearrange("(t p) c -> p t c", p=128)
            d_out[0].go(sp, o_v, X[:, :, :], f)
        for d in d_out:
            if d.count:
                put(sp, None, [(d.sem, d.count)], None)
        for d in (*d_os, *d_ho, *d_s):
            put(sp, None, [(d.sem, d.count)], None)

        block = ctx.enter_context(nc.Block())

        def issue(e, q):
            for waits, fn, inc in e.queue:
                for s, v in waits:
                    q.wait_ge(s, v)
                if fn is not None:
                    ins = fn(q)
                    if inc is not None:
                        ins.then_inc(*inc)

        @block.tensor
        def _(q):
            issue(pe, q)

        @block.vector
        def _(q):
            issue(dve, q)

        @block.scalar
        def _(q):
            issue(act, q)

        @block.gpsimd
        def _(q):
            issue(pool, q)

        @block.sync
        def _(q):
            issue(sp, q)


def places():
    i, j = np.triu_indices(D, k=1)
    return np.where(i < 32, i * D + j, 2048 + (i - 32) * 32 + (j - 32))


def layouts(inp):
    def r(a, *s):
        return np.ascontiguousarray(a).reshape(*s)

    I = {"x": r(inp["x"], B * T, C), "cT": np.ascontiguousarray(np.asarray(inp["cond_1152"]).T)}
    for k, v in inp.items():
        v = np.asarray(v)
        if k in ("x", "cond_1152"):
            continue
        L, n = k[:2], k[8:]
        if k == "L3_cond_P":
            I["PT"] = np.ascontiguousarray(v.T)
        elif k == "L3_cond_W":
            I["L3_WT"] = np.zeros((C, 11 * C), v.dtype)
            I["L3_WT"][:, places()] = v.T
        elif k == "L3_cond_b":
            I["L3_bp"] = np.zeros(11 * C, v.dtype)
            I["L3_bp"][places()] = v
        else:
            I[f"{L}_{n}"] = np.ascontiguousarray(v)
    return I


def make(nc, arrays, stop=None):
    args = {k: nc.dram_tensor(f"in_{k}", a.shape, mybir.dt.from_np(a.dtype), kind="ExternalInput").ap() for k, a in arrays.items()}
    out = nc.dram_tensor("out_0", (B * T, C), F32, kind="ExternalOutput").ap()
    scr_ada = nc.dram_tensor("scr_ada", (3, B, 6 * C), F32, kind="Internal").ap()
    scr_v = nc.dram_tensor("scr_v", (B, 11 * C), F32, kind="Internal").ap()
    scr_o = nc.dram_tensor("scr_o", (B, NH, T, HD), F32, kind="Internal").ap()
    scr_w1 = nc.dram_tensor("scr_w1", (NE, 128, 5, HID), F16, kind="Internal").ap()
    scr_w2 = nc.dram_tensor("scr_w2", (NE, 128, 19, C), F16, kind="Internal").ap()
    program(nc, args, out, scr_ada, scr_v, scr_o, scr_w1, scr_w2, stop)


def kernel(**inputs):
    import concourse.bacc as _bacc
    from concourse.bass_utils import run_bass_kernel_spmd as _run

    nc = _bacc.Bacc("TRN2", target_bir_lowering=False, num_devices=1)
    arrays = layouts(inputs)
    make(nc, arrays)
    r = _run(nc, [{f"in_{k}": a for k, a in arrays.items()}], core_ids=[0])
    return r.results[0]["out_0"].reshape(B, T, C)
```
